# Optimizing a Trainium2 kernel written in Bass

```python
import numpy as np
import jax
import jax.numpy as jnp

def _softmax(x, axis=-1):
    return jax.nn.softmax(x, axis=axis)

def _gelu(x):
    return jax.nn.gelu(x, approximate=True)

def _silu(x):
    return jax.nn.silu(x)

def _sigmoid(x):
    return jax.nn.sigmoid(x)

def _layernorm(x, axis=-1, eps=1e-05):
    m = jnp.mean(x, axis=axis, keepdims=True)
    v = jnp.var(x, axis=axis, keepdims=True)
    return (x - m) / jnp.sqrt(v + eps)

def _scatter_add(tgt, idx, src, axis=0):
    return tgt.at[idx].add(src)

def _segment_sum(src, seg, n):
    return jax.ops.segment_sum(src, seg, n)
kernel_name = 'mk_decoder_preln_d1_seqx_r8_2d640b'

def setup_inputs(seed: int=0):
    np.random.seed(seed)
    _w = jnp.asarray

    def _rec_inputs():
        import jax
        import jax.numpy as jnp
        _rk = jax.random.key(seed)
        x = 0.0001212 + 1 * jax.random.normal(jax.random.fold_in(_rk, 1), (8, 128, 512), jnp.float32)
        _lenS = 128 - jax.random.randint(jax.random.fold_in(_rk, 7), (8,), 0, max(1, 128 // 4) + 1, jnp.int32)
        _lenS2 = 128 - jax.random.randint(jax.random.fold_in(_rk, 8), (8,), 0, max(1, 128 // 4) + 1, jnp.int32)
        _ctx_4096P = jax.random.normal(jax.random.fold_in(_rk, 11), (8, 16, 512), jnp.float32)
        _ctx_4096c = jax.random.dirichlet(jax.random.fold_in(_rk, 511), 0.3 * jnp.ones((16,), jnp.float32), (8, 128))
        _ctx_4096t = jnp.einsum('bsk,bkd->bsd', _ctx_4096c, _ctx_4096P)
        _ctx_4096t = _ctx_4096t * jax.lax.rsqrt(jnp.mean(jnp.square(_ctx_4096t)) + 1e-12) * 0.953939
        ctx_4096 = -0.000125008 + 0.999885 * (_ctx_4096t + 0.3 * jax.random.normal(jax.random.fold_in(_rk, 611), (8, 128, 512), jnp.float32))
        return (x, ctx_4096)
    x, ctx_4096 = _rec_inputs()

    def _L0_attn_setup():
        import jax, jax.numpy as jnp
        import numpy as np
        NUM_HEADS = 32
        NUM_KV_HEADS = 8
        HEAD_DIM = 128
        key = jax.random.key(seed)
        ks = jax.random.split(key, 5)
        B, S, H = (2, 256, 512)
        Dq = NUM_HEADS * HEAD_DIM
        Dkv = NUM_KV_HEADS * HEAD_DIM
        return {'hidden_states': jax.random.normal(ks[0], (B, S, H), jnp.float32), 'w_q': jax.random.normal(ks[1], (H, Dq), jnp.float32) * 0.02, 'w_k': jax.random.normal(ks[2], (H, Dkv), jnp.float32) * 0.02, 'w_v': jax.random.normal(ks[3], (H, Dkv), jnp.float32) * 0.02, 'w_o': jax.random.normal(ks[4], (Dq, H), jnp.float32) * 0.02}
    _L0_attn_all = _L0_attn_setup()
    _L0_attn_in = {k: v for k, v in _L0_attn_all.items() if k in ('w_q', 'w_k', 'w_v', 'w_o')}
    del _L0_attn_all

    def _L0_xattn_setup():
        import jax, jax.numpy as jnp
        import numpy as np
        N, C, S = (16, 64, 512)
        rng = jax.random.key(seed)
        k1, k2, k3 = jax.random.split(rng, 3)
        return {'key': jax.random.normal(k1, (N, C, S), dtype=jnp.float32), 'value': jax.random.normal(k2, (N, C, S), dtype=jnp.float32), 'query': jax.random.normal(k3, (N, C, S), dtype=jnp.float32)}
    _L0_xattn_all = _L0_xattn_setup()
    _L0_xattn_in = {k: v for k, v in _L0_xattn_all.items() if k in ()}
    del _L0_xattn_all

    def _L0_ffn_setup():
        import jax, jax.numpy as jnp
        import numpy as np
        HIDDEN = 512
        INTER = 1376
        GROUPSIZE = 128
        PACK = 8

        def dequant_gptq(qweight, scales, zeros, groupsize):
            K = qweight.shape[0] * PACK
            N = qweight.shape[1]
            k = jnp.arange(K)
            q = qweight[k // PACK, :] >> (k % PACK * 4)[:, None] & 15
            n = jnp.arange(N)
            z = zeros[:, n // PACK] >> (n % PACK * 4)[None, :] & 15
            s = scales.astype(jnp.float32)
            zp = (z.astype(jnp.float32) + 1.0) * s
            g = k // groupsize
            return q.astype(jnp.float32) * s[g] - zp[g]
        key = jax.random.key(seed)
        ks = jax.random.split(key, 11)
        imax = 2147483647
        G_h = HIDDEN // GROUPSIZE
        G_i = (INTER + GROUPSIZE - 1) // GROUPSIZE
        x = (jax.random.normal(ks[0], (2, 256, HIDDEN), dtype=jnp.float32) * 0.5).astype(jnp.float16)
        return {'x': x, 'gate_qweight': jax.random.randint(ks[1], (HIDDEN // PACK, INTER), 0, imax, dtype=jnp.int32), 'gate_scales': (jax.random.uniform(ks[2], (G_h, INTER), dtype=jnp.float32) * 0.01 + 0.001).astype(jnp.float16), 'gate_zeros': jax.random.randint(ks[3], (G_h, INTER // PACK), 0, imax, dtype=jnp.int32), 'up_qweight': jax.random.randint(ks[4], (HIDDEN // PACK, INTER), 0, imax, dtype=jnp.int32), 'up_scales': (jax.random.uniform(ks[5], (G_h, INTER), dtype=jnp.float32) * 0.01 + 0.001).astype(jnp.float16), 'up_zeros': jax.random.randint(ks[6], (G_h, INTER // PACK), 0, imax, dtype=jnp.int32), 'down_qweight': jax.random.randint(ks[7], (INTER // PACK, HIDDEN), 0, imax, dtype=jnp.int32), 'down_scales': (jax.random.uniform(ks[8], (G_i, HIDDEN), dtype=jnp.float32) * 0.01 + 0.001).astype(jnp.float16), 'down_zeros': jax.random.randint(ks[9], (G_i, HIDDEN // PACK), 0, imax, dtype=jnp.int32)}
    _L0_ffn_all = _L0_ffn_setup()
    _L0_ffn_in = {k: v for k, v in _L0_ffn_all.items() if k in ('gate_qweight', 'gate_scales', 'gate_zeros', 'up_qweight', 'up_scales', 'up_zeros', 'down_qweight', 'down_scales', 'down_zeros')}
    del _L0_ffn_all
    return {'x': x, 'ctx_4096': ctx_4096, 'L0_attn_w_q': _L0_attn_in['w_q'], 'L0_attn_w_k': _L0_attn_in['w_k'], 'L0_attn_w_v': _L0_attn_in['w_v'], 'L0_attn_w_o': _L0_attn_in['w_o'], 'L0_ffn_gate_qweight': _L0_ffn_in['gate_qweight'], 'L0_ffn_gate_scales': _L0_ffn_in['gate_scales'], 'L0_ffn_gate_zeros': _L0_ffn_in['gate_zeros'], 'L0_ffn_up_qweight': _L0_ffn_in['up_qweight'], 'L0_ffn_up_scales': _L0_ffn_in['up_scales'], 'L0_ffn_up_zeros': _L0_ffn_in['up_zeros'], 'L0_ffn_down_qweight': _L0_ffn_in['down_qweight'], 'L0_ffn_down_scales': _L0_ffn_in['down_scales'], 'L0_ffn_down_zeros': _L0_ffn_in['down_zeros']}

def reference(x, ctx_4096, L0_attn_w_q, L0_attn_w_k, L0_attn_w_v, L0_attn_w_o, L0_ffn_gate_qweight, L0_ffn_gate_scales, L0_ffn_gate_zeros, L0_ffn_up_qweight, L0_ffn_up_scales, L0_ffn_up_zeros, L0_ffn_down_qweight, L0_ffn_down_scales, L0_ffn_down_zeros):
    import jax
    import jax.numpy as jnp

    def _L0_attn_ref(hidden_states, w_q, w_k, w_v, w_o):
        import jax, jax.numpy as jnp
        import numpy as np
        NUM_HEADS = 32
        NUM_KV_HEADS = 8
        HEAD_DIM = 128
        B, S, _ = hidden_states.shape
        Hq, Hkv, D = (NUM_HEADS, NUM_KV_HEADS, HEAD_DIM)
        g = Hq // Hkv
        scale = D ** (-0.5)
        q = (hidden_states @ w_q).reshape(B, S, Hkv, g, D)
        k = (hidden_states @ w_k).reshape(B, S, Hkv, D)
        v = (hidden_states @ w_v).reshape(B, S, Hkv, D)
        scores = jnp.einsum('bqhgd,bkhd->bhgqk', q, k) * scale
        causal = jnp.tril(jnp.ones((S, S), dtype=bool))
        scores = jnp.where(causal, scores, -jnp.inf)
        probs = jax.nn.softmax(scores.astype(jnp.float32), axis=-1).astype(q.dtype)
        attn = jnp.einsum('bhgqk,bkhd->bqhgd', probs, v)
        attn = attn.reshape(B, S, Hq * D)
        return attn @ w_o

    def _L0_xattn_ref(key, value, query):
        import jax, jax.numpy as jnp
        import numpy as np
        N, C, S = (16, 64, 512)
        KC = key.shape[1]
        sim = jnp.einsum('ncs,nds->ncd', key, query) * KC ** (-0.5)
        sim = jax.nn.softmax(sim, axis=1)
        context = jnp.einsum('ncd,nds->ncs', sim, value)
        return context

    def _L0_ffn_ref(x, gate_qweight, gate_scales, gate_zeros, up_qweight, up_scales, up_zeros, down_qweight, down_scales, down_zeros):
        import jax, jax.numpy as jnp
        import numpy as np
        HIDDEN = 512
        INTER = 1376
        GROUPSIZE = 128
        PACK = 8

        def dequant_gptq(qweight, scales, zeros, groupsize):
            K = qweight.shape[0] * PACK
            N = qweight.shape[1]
            k = jnp.arange(K)
            q = qweight[k // PACK, :] >> (k % PACK * 4)[:, None] & 15
            n = jnp.arange(N)
            z = zeros[:, n // PACK] >> (n % PACK * 4)[None, :] & 15
            s = scales.astype(jnp.float32)
            zp = (z.astype(jnp.float32) + 1.0) * s
            g = k // groupsize
            return q.astype(jnp.float32) * s[g] - zp[g]
        B, S, H = x.shape
        x2 = x.reshape(-1, H).astype(jnp.float32)
        Wg = dequant_gptq(gate_qweight, gate_scales, gate_zeros, GROUPSIZE)
        Wu = dequant_gptq(up_qweight, up_scales, up_zeros, GROUPSIZE)
        Wd = dequant_gptq(down_qweight, down_scales, down_zeros, GROUPSIZE)
        gate = x2 @ Wg
        up = x2 @ Wu
        inter = gate * jax.nn.sigmoid(gate) * up
        out = (inter @ Wd).astype(jnp.float16)
        return out.reshape(B, S, H)
    x = x + _L0_attn_ref(_layernorm(x, axis=-1), L0_attn_w_q, L0_attn_w_k, L0_attn_w_v, L0_attn_w_o)
    x = x + _L0_xattn_ref(ctx_4096, ctx_4096, _layernorm(x, axis=-1))
    x = x + _L0_ffn_ref(_layernorm(x, axis=-1), L0_ffn_gate_qweight, L0_ffn_gate_scales, L0_ffn_gate_zeros, L0_ffn_up_qweight, L0_ffn_up_scales, L0_ffn_up_zeros, L0_ffn_down_qweight, L0_ffn_down_scales, L0_ffn_down_zeros)
    return x

_drawn_inputs = setup_inputs


def setup_inputs(seed=0):
    import zlib

    import numpy as np

    out = dict(_drawn_inputs(seed))
    spreads = {}
    factors = {}
    for name, (base, spread) in spreads.items():
        noise = np.random.default_rng([zlib.crc32(name.encode()), seed]).standard_normal(out[name].shape)
        drawn = base * np.exp(spread * noise) if base else spread * noise
        out[name] = jnp.asarray(drawn.astype(out[name].dtype))
    for name, factor in factors.items():
        out[name] = (out[name] * factor).astype(out[name].dtype)
    return out
```

```python
from contextlib import ExitStack

import concourse.bass as bass
from concourse import mybir

ALU = mybir.AluOpType
ACT = mybir.ActivationFunctionType
AX_X = mybir.AxisListType.X
F32 = mybir.dt.float32
F32R = mybir.dt.float32r
F16 = mybir.dt.float16
I32 = mybir.dt.int32

P = 128
EPS = 1e-5
MASKED = -1e30
NIBBLES = 8
PRIME = 2


def decoder_kernel(nc, x, ctx_in, w_q, w_k, w_v, w_o,
                   gate_q, gate_s, gate_z, up_q, up_s, up_z, down_q, down_s, down_z, out):
    NB, S, H = x.shape
    T = NB * S
    HC = H // P
    NG = w_k.shape[1] // P
    HG = w_q.shape[1] // w_k.shape[1]
    HALF = 512
    NH = T // HALF
    BH = HALF // S
    INTER = gate_q.shape[1]
    NT = (INTER + P - 1) // P
    SCALE = float(P) ** -0.5
    assert S == P and H == HALF and NH == 2 and HG == 4 and NG % 2 == 0

    BLOCKS = [("k", 0, n) for n in range(NH)] + [("v", 0, n) for n in range(NH)]
    BLOCKS += [("q", j, n) for j in range(HG) for n in range(NH)]
    NBLK = len(BLOCKS)
    FILL = {0: [0, 1], 1: [2], 2: [3], 3: [4], 4: [5], 5: [6], 6: [7], 7: [8], 8: [9], 9: [10, 11]}
    SLOTS = NB + 2
    FIRST_UNITS = 2 * 2 + HG
    UNITS = 2 * HG + 2
    SPLIT = {0: ["o0", "o1", "o2", "o3"], 1: ["q0"], 3: ["q1"], 5: ["q2"], 7: ["q3"], 8: ["k"], 9: ["v"]}

    with ExitStack() as stack:
        def sem(name):
            return stack.enter_context(nc.semaphore(name))

        def allocator(scope):
            return lambda name, shape, dt=F32: scope.enter_context(nc.sbuf_tensor(name, shape, dt))

        sb = allocator(stack)
        xacc = sb("xacc", [P, NB, H])
        xn = sb("xn", [P, 2, H])
        ident = sb("ident", [P, P])
        causal = sb("causal", [P, P])
        stats = sb("stats", [P, NB, 6])
        meanvar = sb("meanvar", [P, NB, 2])
        vareps = sb("vareps", [P, NB])
        std = sb("std", [P, NB])
        rstd = sb("rstd", [P, NB])
        newton = sb("newton", [P, NB])
        rowmax = sb("rowmax", [P, 2, HG])
        negmax = sb("negmax", [P, 2, HG])
        rowsum = sb("rowsum", [P, 2, HG])
        rowinv = sb("rowinv", [P, 2, HG])
        part_i = sb("part_i", [P, 1], I32)
        q_shift = sb("q_shift", [P, 1], I32)
        z_shift = sb("z_shift", [P, NIBBLES], I32)
        psum = stack.enter_context(nc.psum_tensor("psum", [P, 8, HALF], F32))
        BK_S, BK_T, BK_PV, BK_O, BK_VT, BK_PROJ = 0, 1, 2, 3, 4, (5, 6)

        with ExitStack() as scope:
            sb = allocator(scope)
            xt_hi = sb("xt_hi", [P, HC, T], F32R)
            xt_lo = sb("xt_lo", [P, HC, T], F32R)
            wq_hi = sb("wq_hi", [P, HG, HC, P], F32R)
            wq_lo = sb("wq_lo", [P, HG, HC, P], F32R)
            wk_hi = sb("wk_hi", [P, HC, P], F32R)
            wk_lo = sb("wk_lo", [P, HC, P], F32R)
            wv_hi = sb("wv_hi", [P, HC, P], F32R)
            wv_lo = sb("wv_lo", [P, HC, P], F32R)
            wo_hi = sb("wo_hi", [P, HG, H], F32R)
            wo_lo = sb("wo_lo", [P, HG, H], F32R)
            wq_raw = sb("wq_raw", [P, HC, HG * P])
            wk_raw = sb("wk_raw", [P, HC, P])
            wv_raw = sb("wv_raw", [P, HC, P])
            wo_raw = sb("wo_raw", [P, HG, H])
            qt = [sb(f"qt{i}", [P, HG, T]) for i in range(2)]
            kt = [sb(f"kt{i}", [P, T]) for i in range(2)]
            vt = sb("vt", [P, HALF])
            v_hi = [sb(f"v_hi{i}", [P, NB, P], F32R) for i in range(2)]
            v_lo = [sb(f"v_lo{i}", [P, NB, P], F32R) for i in range(2)]
            probs = sb("probs", [P, 2, HG, P])
            pt_hi = sb("pt_hi", [P, HG, P], F32R)
            pt_lo = sb("pt_lo", [P, HG, P], F32R)
            at_hi = sb("at_hi", [P, 2, HG, P], F32R)
            at_lo = sb("at_lo", [P, 2, HG, P], F32R)
        with ExitStack() as scope:
            sb = allocator(scope)
            cx = sb("cx", [P, NB, H])
            cxt = sb("cxt", [P, HC, T])
            query_t = sb("query_t", [P, 2, HC, P])
            xprobs = sb("xprobs", [P, 2, P])
        with ExitStack() as scope:
            sb = allocator(scope)
            int_hi = sb("int_hi", [P, NT, T], F32R)
            int_lo = sb("int_lo", [P, NT, T], F32R)
            ft_hi = sb("ft_hi", [P, HC, T], F32R)
            ft_lo = sb("ft_lo", [P, HC, T], F32R)
            f_q = sb("f_q", [P, 2, 2, HC, P], I32)
            f_z = sb("f_z", [P, 2, 2, HC, P // NIBBLES], I32)
            f_s = sb("f_s", [P, 2, 2, HC, P], F16)
            f_zn = sb("f_zn", [P, HC, P], I32)
            f_m = sb("f_m", [P, 2, HC, P])
            f_w = sb("f_w", [P, 2, HC, P])
            f_hi = sb("f_hi", [P, 2, 2, HC, P], F32R)
            f_lo = sb("f_lo", [P, 2, 2, HC, P], F32R)
            f_sig = sb("f_sig", [P, T])
            f_int = sb("f_int", [P, T])
            y16 = sb("y16", [P, 2, H], F16)

        ld_x = [sem(f"ld_x{b}") for b in range(NB)]
        ld_w = {k: sem(f"ld_w{k}") for k in "qkvo"}
        ld_cx = sem("ld_cx")
        consts_pool = sem("consts_pool")
        consts_dve = sem("consts_dve")
        stat_step = sem("stat_step")
        var_ready = sem("var_ready")
        std_ready = sem("std_ready")
        ln_ready = [sem(f"ln_ready{i}") for i in range(3)]
        ln_turned = [sem(f"ln_turned{i}") for i in range(3)]
        ln_hi = [sem(f"ln_hi{i}") for i in range(3)]
        ln_lo = [sem(f"ln_lo{i}") for i in range(3)]
        w_hi = sem("w_hi")
        w_lo = sem("w_lo")
        proj_done = sem("proj_done")
        proj_out = sem("proj_out")
        vt_done = sem("vt_done")
        vt_hi = sem("vt_hi")
        vt_lo = sem("vt_lo")
        score_done = sem("score_done")
        masked = sem("masked")
        maxed = sem("maxed")
        neg_ready = sem("neg_ready")
        exp_done = sem("exp_done")
        inv_ready = sem("inv_ready")
        prob_ready = sem("prob_ready")
        pt_done = sem("pt_done")
        pthi_ready = sem("pthi_ready")
        ptlo_ready = sem("ptlo_ready")
        pv_done = sem("pv_done")
        athi_ready = sem("athi_ready")
        atlo_ready = sem("atlo_ready")
        o_done = sem("o_done")
        o_added = sem("o_added")
        xs_done = sem("xs_done")
        xs_max = sem("xs_max")
        xs_neg = sem("xs_neg")
        xs_exp = sem("xs_exp")
        xs_inv = sem("xs_inv")
        xs_prob = sem("xs_prob")
        xc_done = sem("xc_done")
        x_added = sem("x_added")
        ld_f = [sem(f"ld_f{i}") for i in range(2)]
        fq_step = sem("fq_step")
        fm_ready = sem("fm_ready")
        fw_ready = sem("fw_ready")
        fhi_ready = sem("fhi_ready")
        flo_ready = sem("flo_ready")
        gu_done = sem("gu_done")
        sig_ready = sem("sig_ready")
        gs_ready = sem("gs_ready")
        int_ready = sem("int_ready")
        inthi_ready = sem("inthi_ready")
        intlo_ready = sem("intlo_ready")
        down_done = sem("down_done")
        y16_ready = sem("y16_ready")
        y_ready = sem("y_ready")
        stored = sem("stored")

        CTX_BLOCKS = NG * NBLK
        W_SPLITS = FIRST_UNITS + UNITS * NG - 2 * 2 - HG
        LAST = NG - 1
        ATT = NG * NB

        def units_before(g):
            return g * UNITS + FIRST_UNITS - (2 if isinstance(g, int) and g == LAST else 0)

        def width(n):
            return min(P, INTER - n * P)

        block = stack.enter_context(nc.Block())

        @block.sync
        def _(sp):
            wq_v = w_q.rearrange("(c p) n -> p c n", p=P)
            wk_v = w_k.rearrange("(c p) n -> p c n", p=P)
            wv_v = w_v.rearrange("(c p) n -> p c n", p=P)
            wo_v = w_o.rearrange("(h p) n -> p h n", p=P)

            def load_w(kind, g):
                dst, src = {
                    "q": (wq_raw, lambda: wq_v[:, :, g * HG * P:(g + 1) * HG * P]),
                    "k": (wk_raw, lambda: wk_v[:, :, g * P:(g + 1) * P]),
                    "v": (wv_raw, lambda: wv_v[:, :, g * P:(g + 1) * P]),
                    "o": (wo_raw, lambda: wo_v[:, g * HG:(g + 1) * HG, :]),
                }[kind]
                sp.dma_start(dst[:], src()).then_inc(ld_w[kind], 16)

            for b in range(NB):
                sp.dma_start(xacc[:, b, :], x[b]).then_inc(ld_x[b], 16)
                if b == BH - 1:
                    load_w("k", 0)
                    load_w("v", 0)
            load_w("q", 0)
            load_w("o", 0)
            sp.wait_ge(w_lo, 1)
            load_w("k", 1)
            sp.wait_ge(w_lo, 2)
            load_w("v", 1)
            sp.wait_ge(w_lo, 2 + HG)
            load_w("q", 1)
            for g in range(NG):
                n = units_before(g)
                if g + 2 < NG:
                    sp.wait_ge(w_lo, n)
                    load_w("k", g + 2)
                    load_w("v", g + 2)
                if g + 1 < NG:
                    sp.wait_ge(w_lo, n + HG)
                    load_w("o", g + 1)
                if g + 2 < NG:
                    sp.wait_ge(w_lo, n + 2 * HG)
                    load_w("q", g + 2)
            sp.wait_ge(proj_done, CTX_BLOCKS)
            sp.dma_start(cx[:], ctx_in.rearrange("b c s -> c b s")).then_inc(ld_cx, 16)

            def load_ffn(n):
                r, c0, w = n % 2, n * P, width(n)
                for m, (q, s, z) in enumerate(((gate_q, gate_s, gate_z), (up_q, up_s, up_z))):
                    for c in range(HC):
                        rows = q[c * P // NIBBLES:(c + 1) * P // NIBBLES, c0:c0 + w]
                        sp.dma_start(f_q[:, r, m, c, 0:w],
                                     rows.unsqueeze(1).to_broadcast([P // NIBBLES, NIBBLES, w])
                                     ).then_inc(ld_f[r], 16)
                    sp.dma_start(f_s[:, r, m, :, 0:w],
                                 s[:, c0:c0 + w].unsqueeze(0).to_broadcast([P, HC, w])).then_inc(ld_f[r], 16)
                    zc, zw = c0 // NIBBLES, w // NIBBLES
                    sp.dma_start(f_z[:, r, m, :, 0:zw],
                                 z[:, zc:zc + zw].unsqueeze(0).to_broadcast([P, HC, zw])).then_inc(ld_f[r], 16)

            def load_down(c):
                r, w = (NT + c) % 2, width(c)
                rows = down_q[c * P // NIBBLES:(c * P + w) // NIBBLES, :]
                sp.dma_start(f_q[0:w, r, 0].rearrange("p a b -> p (a b)"),
                             rows.unsqueeze(1).to_broadcast([w // NIBBLES, NIBBLES, H])).then_inc(ld_f[r], 16)
                sp.dma_start(f_s[0:w, r, 0].rearrange("p a b -> p (a b)"),
                             down_s[c:c + 1, :].to_broadcast([w, H])).then_inc(ld_f[r], 16)
                sp.dma_start(f_z[0:w, r, 0].rearrange("p a b -> p (a b)"),
                             down_z[c:c + 1, :].to_broadcast([w, H // NIBBLES])).then_inc(ld_f[r], 16)

            sp.wait_ge(o_done, ATT + PRIME)
            load_ffn(0)
            load_ffn(1)
            for n in range(2, NT):
                sp.wait_ge(fm_ready, 2 * (n - 1))
                sp.wait_ge(fw_ready, 2 * (n - 1))
                load_ffn(n)
            for c in range(NT):
                done = 2 * (NT - 1) if c == 0 else 2 * NT + c - 1
                sp.wait_ge(fm_ready, done)
                sp.wait_ge(fw_ready, done)
                load_down(c)
            for b in range(NB):
                sp.wait_ge(y_ready, b + 1)
                sp.dma_start(out[b], xacc[:, b, :]).then_inc(stored, 16)
            sp.wait_ge(stored, 16 * NB)

        @block.tensor
        def _(pe):
            for s in (score_done, pt_done, pv_done, o_done, gu_done):
                pe.sem_inc(s, PRIME)

            def passes(dst, a_hi, a_lo, b_hi, b_lo, start, stop):
                pe.matmul(dst, a_hi, b_hi, start=start, stop=False)
                pe.matmul(dst, a_hi, b_lo, start=False, stop=False)
                return pe.matmul(dst, a_lo, b_hi, start=False, stop=stop)

            def turn_tile(bank, src):
                for c in range(HC):
                    mm = pe.transpose(psum[:, bank, c * P:(c + 1) * P], src[:, c * P:(c + 1) * P], ident[:])
                return mm

            def project(g, i):
                kind, j, n = BLOCKS[i]
                hi, lo = {"k": (wk_hi[:], wk_lo[:]), "v": (wv_hi[:], wv_lo[:]),
                          "q": (wq_hi[:, j], wq_lo[:, j])}[kind]
                dst = psum[:, BK_PROJ[i % 2], :]
                for c in range(HC):
                    cols = slice(n * HALF, (n + 1) * HALF)
                    mm = passes(dst, hi[:, c, :], lo[:, c, :], xt_hi[:, c, cols], xt_lo[:, c, cols],
                                c == 0, c == HC - 1)
                mm.then_inc(proj_done, 1)

            def turn_v(g, n):
                pe.wait_ge(proj_out, g * NBLK + 3 + n)
                if not (isinstance(g, int) and g == 0 and n == 0):
                    pe.wait_ge(vt_lo, g * NH + n)
                for k in range(BH):
                    mm = pe.transpose(psum[:, BK_VT, k * P:(k + 1) * P], vt[:, k * P:(k + 1) * P], ident[:])
                mm.then_inc(vt_done, 1)

            pe.wait_ge(consts_pool, 4)
            for b in range(NB):
                pe.wait_ge(ln_ready[0], b + 1)
                if b >= 2:
                    pe.wait_ge(ln_lo[0], b - 1)
                turn_tile((BK_T, BK_VT)[b % 2], xn[:, b % 2, :]).then_inc(ln_turned[0], 1)
            for i in range(NBLK):
                kind, j, n = BLOCKS[i]
                pe.wait_ge(ln_lo[0], BH if n == 0 and i == 0 else NB)
                pe.wait_ge(w_lo, {"k": 1, "v": 2, "q": 3 + j}[kind])
                if i >= 2:
                    pe.wait_ge(proj_out, i - 1)
                if i == 3:
                    turn_v(0, 0)
                if i == 4:
                    turn_v(0, 1)
                project(0, i)

            def group(g, p, more):
                step = g * NB
                for t in range(SLOTS):
                    if t < NB:
                        pe.wait_ge(masked, step + t + PRIME)
                        pe.wait_ge(proj_out, (g + 1) * NBLK - (1 if t < BH else 0))
                        for j in range(HG):
                            mm = pe.matmul(psum[:, BK_S, j * P:(j + 1) * P],
                                           qt[p][:, j, t * P:(t + 1) * P], kt[p][:, t * P:(t + 1) * P],
                                           start=True, stop=True)
                        mm.then_inc(score_done, 1)
                    if 1 <= t <= NB:
                        u = t - 1
                        pe.wait_ge(prob_ready, step + u + 1)
                        pe.wait_ge(ptlo_ready, step + u + PRIME)
                        for j in range(HG):
                            mm = pe.transpose(psum[:, BK_T, j * P:(j + 1) * P], probs[:, u % 2, j, :], ident[:])
                        mm.then_inc(pt_done, 1)
                    if more:
                        for i in FILL[t]:
                            kind, j, n = BLOCKS[i]
                            if i == 3:
                                turn_v(g + 1, 0)
                            if i == 4:
                                turn_v(g + 1, 1)
                            ready = {"k": FIRST_UNITS - 1, "v": FIRST_UNITS, "q": FIRST_UNITS + HG + 1 + j}[kind]
                            pe.wait_ge(w_lo, g * UNITS + ready)
                            pe.wait_ge(proj_out, (g + 1) * NBLK + i - 1)
                            project(g + 1, i)
                    elif t >= 2:
                        b = t - 2
                        if b == 0:
                            pe.wait_ge(ld_cx, 16)
                        pe.wait_ge(proj_out, CTX_BLOCKS + b - 1)
                        turn_tile(BK_PROJ[b % 2], cx[:, b, :]).then_inc(proj_done, 1)
                    if 1 <= t <= NB:
                        u = t - 1
                        pe.wait_ge(ptlo_ready, step + u + 1 + PRIME)
                        pe.wait_ge(vt_lo, g * NH + (1 if u < BH else 2))
                        pe.wait_ge(atlo_ready, step + u + PRIME)
                        passes(psum[:, BK_PV, :], v_hi[p][:, u, :], v_lo[p][:, u, :],
                               pt_hi[:].rearrange("p a b -> p (a b)"), pt_lo[:].rearrange("p a b -> p (a b)"),
                               True, True).then_inc(pv_done, 1)
                    if t >= 2:
                        u = t - 2
                        pe.wait_ge(atlo_ready, step + u + 1 + PRIME)
                        pe.wait_ge(w_lo, units_before(g) + HG)
                        pe.wait_ge(o_added, step + u + PRIME)
                        for j in range(HG):
                            mm = passes(psum[:, BK_O, :], at_hi[:, u % 2, j, :], at_lo[:, u % 2, j, :],
                                        wo_hi[:, j, :], wo_lo[:, j, :], j == 0, j == HG - 1)
                        mm.then_inc(o_done, 1)

            with pe.Fori(0, NG // 2 - 1) as pair:
                for p in range(2):
                    group(pair * 2 + p, p, True)
            group(NG - 2, 0, True)
            group(NG - 1, 1, False)

            for i in range(NB + 2):
                if i < NB:
                    pe.wait_ge(ln_ready[1], i + 1)
                    if i >= 2:
                        pe.wait_ge(ln_hi[1], i - 1)
                    turn_tile((BK_T, BK_VT)[i % 2], xn[:, i % 2, :]).then_inc(ln_turned[1], 1)
                if 1 <= i <= NB:
                    b = i - 1
                    pe.wait_ge(ln_hi[1], b + 1)
                    pe.wait_ge(proj_out, CTX_BLOCKS + b + 1)
                    if b >= 2:
                        pe.wait_ge(xs_exp, b - 1)
                    else:
                        pe.wait_ge(masked, ATT + PRIME)
                        pe.wait_ge(atlo_ready, ATT + PRIME)
                    for c in range(HC):
                        mm = pe.matmul(psum[:, (BK_S, BK_PV)[b % 2], 0:P], query_t[:, b % 2, c, :],
                                       cxt[:, c, b * P:(b + 1) * P], start=(c == 0), stop=(c == HC - 1))
                    mm.then_inc(xs_done, 1)
                if i >= 2:
                    b = i - 2
                    pe.wait_ge(xs_prob, b + 1)
                    if b >= 2:
                        pe.wait_ge(x_added, b - 1)
                    pe.matmul(psum[:, BK_PROJ[b % 2], :], xprobs[:, b % 2, :], cx[:, b, :],
                              start=True, stop=True).then_inc(xc_done, 1)
            for b in range(NB):
                pe.wait_ge(ln_ready[2], b + 1)
                if b >= 2:
                    pe.wait_ge(ln_lo[2], b - 1)
                turn_tile((BK_T, BK_VT)[b % 2], xn[:, b % 2, :]).then_inc(ln_turned[2], 1)
            pe.wait_ge(ln_lo[2], NB)

            def gate_up(n, r, w):
                for m in range(2):
                    pe.wait_ge(flo_ready, n * 2 + m + 1)
                    if m == 0:
                        pe.wait_ge(int_ready, n + PRIME - 1)
                    for h in range(NH):
                        for c in range(HC):
                            cols = slice(h * HALF, (h + 1) * HALF)
                            mm = passes(psum[0:w, 4 * r + 2 * m + h, :], f_hi[:, r, m, c, 0:w],
                                        f_lo[:, r, m, c, 0:w], ft_hi[:, c, cols], ft_lo[:, c, cols],
                                        c == 0, c == HC - 1)
                    mm.then_inc(gu_done, 1)

            with pe.Fori(0, (NT - 3) // 2) as pair:
                for r in range(2):
                    gate_up(pair * 2 + r, r, P)
            for n in range(NT - 3, NT):
                gate_up(n, n % 2, width(n))

            for c in range(NT):
                w, r = width(c), (NT + c) % 2
                pe.wait_ge(flo_ready, 2 * NT + c + 1)
                pe.wait_ge(intlo_ready, c + 1 + PRIME)
                for k in range(NB):
                    b = (k + BH) % NB if c == 0 else k
                    if c == 0 and k == 0:
                        pe.wait_ge(int_ready, NT - 1 + PRIME)
                    if c == 0 and b == 0:
                        pe.wait_ge(int_ready, NT + PRIME)
                    mm = passes(psum[:, b, :], int_hi[0:w, c, b * P:(b + 1) * P], int_lo[0:w, c, b * P:(b + 1) * P],
                                f_hi[0:w, r, 0].rearrange("p a b -> p (a b)"),
                                f_lo[0:w, r, 0].rearrange("p a b -> p (a b)"), c == 0, c == NT - 1)
                    if c == NT - 1:
                        mm.then_inc(down_done, 1)
                if c < NT - 1:
                    mm.then_inc(gu_done, 1)

        @block.scalar
        def _(act):
            def split_first(unit, g):
                kind, j = unit[0], int(unit[1:] or 0)
                raw, hi = {
                    "k": lambda: (wk_raw[:], wk_hi[:]), "v": lambda: (wv_raw[:], wv_hi[:]),
                    "q": lambda: (wq_raw[:, :, j * P:(j + 1) * P], wq_hi[:, j]),
                    "o": lambda: (wo_raw[:, j], wo_hi[:, j]),
                }[kind]()
                act.copy(hi, raw).then_inc(w_hi, 1)

            def std_of_var(k):
                act.wait_ge(var_ready, k + 1)
                act.activation(std[:], vareps[:], ACT.Sqrt).then_inc(std_ready, 1)

            std_of_var(0)
            act.wait_ge(ld_w["k"], 16)
            split_first("k", 0)
            act.wait_ge(ld_w["v"], 16)
            split_first("v", 0)
            for b in range(NB):
                act.wait_ge(ln_turned[0], b + 1)
                act.copy(xt_hi[:, :, b * P:(b + 1) * P],
                         psum[:, (BK_T, BK_VT)[b % 2], :].rearrange("p (c t) -> p c t", c=HC)
                         ).then_inc(ln_hi[0], 1)
            act.wait_ge(ld_w["q"], 16)
            for j in range(HG):
                split_first(f"q{j}", 0)

            def project_out(g, i, p):
                kind, j, n = BLOCKS[i]
                act.wait_ge(proj_done, g * NBLK + i + 1)
                cols = slice(n * HALF, (n + 1) * HALF)
                if kind == "v":
                    if not (isinstance(g, int) and g == 0 and n == 0):
                        act.wait_ge(vt_done, g * NH + n)
                    dst = vt[:]
                else:
                    dst = kt[p][:, cols] if kind == "k" else qt[p][:, j, cols]
                act.copy(dst, psum[:, BK_PROJ[i % 2], :]).then_inc(proj_out, 1)

            def v_first(g, n, p):
                act.wait_ge(vt_done, g * NH + n + 1)
                act.copy(v_hi[p][:, n * BH:(n + 1) * BH, :],
                         psum[:, BK_VT, :].rearrange("p (a b) -> p a b", a=BH)).then_inc(vt_hi, 1)

            for i in range(NBLK):
                if i == 4:
                    v_first(0, 1, 0)
                project_out(0, i, 0)
                if i == 2:
                    v_first(0, 0, 0)
                if i == 5:
                    act.wait_ge(ld_w["k"], 32)
                    split_first("k", 1)
                    act.wait_ge(ld_w["v"], 32)
                    split_first("v", 1)

            def group(g, p, more, more2):
                step = g * NB
                for t in range(SLOTS):
                    if 1 <= t <= NB:
                        u = t - 1
                        act.wait_ge(pt_done, step + u + 1 + PRIME)
                        act.wait_ge(pv_done, step + u + PRIME)
                        act.copy(pt_hi[:], psum[:, BK_T, :].rearrange("p (a b) -> p a b", a=HG)
                                 ).then_inc(pthi_ready, 1)
                    if t < NB:
                        act.wait_ge(neg_ready, step + t + 1)
                        for j in range(HG):
                            e = act.activation(probs[:, t % 2, j, :], probs[:, t % 2, j, :], ACT.Exp,
                                               bias=negmax[:, t % 2, j:j + 1], scale=SCALE,
                                               accum_out=rowsum[:, t % 2, j:j + 1])
                        e.then_inc(exp_done, 1)
                    if more:
                        for i in FILL[t]:
                            if i == 0:
                                act.wait_ge(score_done, step + PRIME)
                                act.wait_ge(pv_done, step + PRIME)
                            project_out(g + 1, i, 1 - p)
                            if i == 2:
                                v_first(g + 1, 0, 1 - p)
                            if i == 3:
                                v_first(g + 1, 1, 1 - p)
                    elif t >= 2:
                        b = t - 2
                        act.wait_ge(proj_done, CTX_BLOCKS + b + 1)
                        act.copy(cxt[:, :, b * P:(b + 1) * P],
                                 psum[:, BK_PROJ[b % 2], :].rearrange("p (c t) -> p c t", c=HC)
                                 ).then_inc(proj_out, 1)
                    if 1 <= t <= NB:
                        u = t - 1
                        act.wait_ge(pv_done, step + u + 1 + PRIME)
                        act.wait_ge(o_done, step + u - 1 + PRIME)
                        act.copy(at_hi[:, u % 2], psum[:, BK_PV, :].rearrange("p (a b) -> p a b", a=HG)
                                 ).then_inc(athi_ready, 1)
                    for unit in SPLIT.get(t, ()):
                        kind, j = unit[0], int(unit[1:] or 0)
                        if kind == "o":
                            if j == 0:
                                act.wait_ge(ld_w["o"], g * 16 + 16)
                                act.wait_ge(o_done, step + PRIME)
                            split_first(unit, g)
                        if kind == "q" and more:
                            act.wait_ge(ld_w["q"], g * 16 + 32)
                            act.wait_ge(proj_done, g * NBLK + 4 + NH * (j + 1))
                            split_first(unit, g + 1)
                        if kind in "kv" and more2:
                            act.wait_ge(ld_w[kind], g * 16 + 48)
                            used = NH if kind == "k" else 2 * NH
                            act.wait_ge(proj_done, (g + 1) * NBLK + used)
                            split_first(unit, g + 2)

            with act.Fori(0, NG // 2 - 1) as pair:
                for p in range(2):
                    group(pair * 2 + p, p, True, True)
            group(NG - 2, 0, True, False)
            group(NG - 1, 1, False, False)

            std_of_var(1)
            for i in range(NB + 1):
                if i < NB:
                    act.wait_ge(ln_turned[1], i + 1)
                    if i >= 2:
                        act.wait_ge(xs_done, i - 1)
                    act.copy(query_t[:, i % 2], psum[:, (BK_T, BK_VT)[i % 2], :].rearrange("p (c t) -> p c t", c=HC)
                             ).then_inc(ln_hi[1], 1)
                if i >= 1:
                    b = i - 1
                    act.wait_ge(xs_neg, b + 1)
                    if b >= 2:
                        act.wait_ge(xc_done, b - 1)
                    act.activation(xprobs[:, b % 2, :], psum[:, (BK_S, BK_PV)[b % 2], 0:P], ACT.Exp,
                                   bias=negmax[:, b % 2, 0:1], scale=SCALE,
                                   accum_out=rowsum[:, b % 2, 0:1]).then_inc(xs_exp, 1)
            std_of_var(2)

            def weight_first(unit, r, m, before, w):
                act.wait_ge(fw_ready, unit + 1)
                act.wait_ge(gu_done, before + PRIME)
                act.copy(f_hi[:, r, m, :, 0:w], f_w[:, m, :, 0:w]).then_inc(fhi_ready, 1)

            def tile_weights(n, r, w):
                for m in range(2):
                    weight_first(n * 2 + m, r, m, n * 2 + m - 3, w)

            def down_weights(c):
                w, r, m = width(c), (NT + c) % 2, 0
                act.wait_ge(fw_ready, 2 * NT + c + 1)
                act.wait_ge(gu_done, (2 * (NT - 2 + c) + 1 if c < 2 else 2 * NT + c - 1) + PRIME)
                act.copy(f_hi[0:w, r, 0], f_w[0:w, c % 2]).then_inc(fhi_ready, 1)

            def inner(n, w):
                act.wait_ge(gu_done, n * 2 + 1 + PRIME)
                act.wait_ge(int_ready, n + PRIME)
                gate = psum[0:w, 4 * inner.r:4 * inner.r + 2, :].rearrange("p a b -> p (a b)")
                act.activation(f_sig[0:w, :], gate, ACT.Sigmoid).then_inc(sig_ready, 1)

            def inner_first(n, w):
                act.wait_ge(int_ready, n + 1 + PRIME)
                act.copy(int_hi[0:w, bass.ds(n, 1), :].rearrange("p a b -> p (a b)"),
                         f_int[0:w, :]).then_inc(inthi_ready, 1)

            for m in range(2):
                act.wait_ge(fw_ready, m + 1)
                act.copy(f_hi[:, 0, m], f_w[:, m]).then_inc(fhi_ready, 1)
            for b in range(NB):
                act.wait_ge(ln_turned[2], b + 1)
                act.copy(ft_hi[:, :, b * P:(b + 1) * P],
                         psum[:, (BK_T, BK_VT)[b % 2], :].rearrange("p (c t) -> p c t", c=HC)
                         ).then_inc(ln_hi[2], 1)

            with act.Fori(0, (NT - 3) // 2) as pair:
                for r in range(2):
                    n = pair * 2 + r
                    tile_weights(n + 1, 1 - r, P)
                    inner.r = r
                    inner(n, P)
                    inner_first(n, P)
            for n in range(NT - 3, NT):
                if n + 1 < NT:
                    tile_weights(n + 1, (n + 1) % 2, width(n + 1))
                else:
                    down_weights(0)
                inner.r = n % 2
                inner(n, width(n))
                inner_first(n, width(n))
            for c in range(1, NT):
                down_weights(c)
            for b in range(NB):
                act.wait_ge(down_done, b + 1)
                if b >= 2:
                    act.wait_ge(y_ready, b - 1)
                act.copy(y16[:, b % 2, :], psum[:, b, :]).then_inc(y16_ready, 1)

        @block.gpsimd
        def _(pool):
            pool.memset(ident[:], 0.0).then_inc(consts_pool, 1)
            pool.memset(causal[:], 0.0).then_inc(consts_pool, 1)
            pool.wait_ge(consts_pool, 2)
            pool.affine_select(out=ident[:], in_=ident[:], compare_op=ALU.not_equal, fill=1.0,
                               base=0, pattern=[[-1, P]], channel_multiplier=1).then_inc(consts_pool, 1)
            pool.affine_select(out=causal[:], in_=causal[:], compare_op=ALU.is_ge, fill=MASKED,
                               base=0, pattern=[[-1, P]], channel_multiplier=1).then_inc(consts_pool, 1)
            pool.iota(part_i[:], pattern=[[0, 1]], base=0, channel_multiplier=1).then_inc(consts_pool, 1)
            pool.iota(z_shift[:], pattern=[[4, NIBBLES]], base=0, channel_multiplier=0).then_inc(consts_pool, 1)
            pool.sem_inc(intlo_ready, PRIME)

            def split_second(unit, count):
                kind, j = unit[0], int(unit[1:] or 0)
                raw, hi, lo = {
                    "k": lambda: (wk_raw[:], wk_hi[:], wk_lo[:]), "v": lambda: (wv_raw[:], wv_hi[:], wv_lo[:]),
                    "q": lambda: (wq_raw[:, :, j * P:(j + 1) * P], wq_hi[:, j], wq_lo[:, j]),
                    "o": lambda: (wo_raw[:, j], wo_hi[:, j], wo_lo[:, j]),
                }[kind]()
                pool.wait_ge(w_hi, count)
                pool.tensor_tensor(lo, raw, hi.bitcast(F32), ALU.subtract).then_inc(w_lo, 1)

            for n, unit in enumerate(["k", "v", "q0", "q1", "q2", "q3", "k", "v"]):
                split_second(unit, n + 1)

            def group(g, more, more2):
                step = g * NB
                n = 0
                for t in range(SLOTS):
                    if t < NB:
                        pool.wait_ge(inv_ready, step + t + 1)
                        pool.tensor_tensor(probs[:, t % 2], probs[:, t % 2],
                                           rowinv[:, t % 2, :].unsqueeze(2).to_broadcast([P, HG, P]),
                                           ALU.mult).then_inc(prob_ready, 1)
                    for unit in SPLIT.get(t, ()):
                        if unit[0] == "o" or (unit[0] == "q" and more) or (unit[0] in "kv" and more2):
                            n += 1
                            split_second(unit, units_before(g) + n)

            with pool.Fori(0, NG // 2 - 1) as pair:
                for p in range(2):
                    group(pair * 2 + p, True, True)
            group(NG - 2, True, False)
            group(NG - 1, False, False)

            def weights(unit, m, r, w, free=True):
                pool.wait_ge(fm_ready, unit + 1)
                if free:
                    pool.wait_ge(flo_ready, unit - 1)
                pool.tensor_tensor(f_w[:, m, :, 0:w], f_m[:, m, :, 0:w], f_s[:, r, m, :, 0:w],
                                   ALU.mult).then_inc(fw_ready, 1)
                pool.wait_ge(fhi_ready, unit + 1)
                pool.tensor_tensor(f_lo[:, r, m, :, 0:w], f_w[:, m, :, 0:w],
                                   f_hi[:, r, m, :, 0:w].bitcast(F32), ALU.subtract).then_inc(flo_ready, 1)

            def down_weights(c):
                w, r, unit, m = width(c), (NT + c) % 2, 2 * NT + c, c % 2
                pool.wait_ge(fm_ready, unit + 1)
                pool.wait_ge(flo_ready, unit - 1)
                pool.tensor_tensor(f_w[0:w, m], f_m[0:w, m], f_s[0:w, r, 0], ALU.mult).then_inc(fw_ready, 1)
                pool.wait_ge(fhi_ready, unit + 1)
                pool.tensor_tensor(f_lo[0:w, r, 0], f_w[0:w, m], f_hi[0:w, r, 0].bitcast(F32),
                                   ALU.subtract).then_inc(flo_ready, 1)

            def inner_second(n, w):
                pool.wait_ge(inthi_ready, n + 1)
                at = bass.ds(n, 1)
                pool.tensor_tensor(int_lo[0:w, at, :].rearrange("p a b -> p (a b)"), f_int[0:w, :],
                                   int_hi[0:w, at, :].rearrange("p a b -> p (a b)").bitcast(F32),
                                   ALU.subtract).then_inc(intlo_ready, 1)

            for m in range(2):
                weights(m, m, 0, P, free=False)
            with pool.Fori(0, (NT - 3) // 2) as pair:
                for r in range(2):
                    n = pair * 2 + r
                    for m in range(2):
                        weights((n + 1) * 2 + m, m, 1 - r, P)
                    inner_second(n, P)
            for n in range(NT - 3, NT):
                if n + 1 < NT:
                    for m in range(2):
                        weights((n + 1) * 2 + m, m, (n + 1) % 2, width(n + 1))
                else:
                    down_weights(0)
                inner_second(n, width(n))
            for c in range(1, NT):
                down_weights(c)

        @block.vector
        def _(dve):
            for s in (masked, ptlo_ready, atlo_ready, o_added, int_ready):
                dve.sem_inc(s, PRIME)
            steps = [0]

            def after(ins):
                steps[0] += 1
                ins.then_inc(stat_step, 1)
                dve.wait_ge(stat_step, steps[0])

            def count(b):
                after(dve.bn_stats(stats[:, b, :], xacc[:, b, :]))
                dve.bn_aggr(meanvar[:, b, :], stats[:, b:b + 1, :].rearrange("p a b -> p (a b)")
                            ).then_inc(stat_step, 1)
                steps[0] += 1

            def inverse_deviation(k):
                dve.wait_ge(stat_step, steps[0])
                dve.tensor_scalar(vareps[:], meanvar[:, :, 1], EPS, None, ALU.add).then_inc(var_ready, 1)
                dve.wait_ge(std_ready, k + 1)
                after(dve.reciprocal(rstd[:], std[:]))
                after(dve.tensor_tensor(newton[:], rstd[:], rstd[:], ALU.mult))
                after(dve.tensor_tensor(newton[:], newton[:], vareps[:], ALU.mult))
                after(dve.tensor_scalar(newton[:], newton[:], -0.5, 1.5, ALU.mult, ALU.add))
                after(dve.tensor_tensor(rstd[:], rstd[:], newton[:], ALU.mult))

            def normalise(b, k):
                dve.tensor_scalar(xn[:, b % 2, :], xacc[:, b, :], meanvar[:, b, 0:1], rstd[:, b:b + 1],
                                  ALU.subtract, ALU.mult).then_inc(ln_ready[k], 1)

            def tile_second(b, k, hi, lo):
                dve.wait_ge(ln_hi[k], b + 1)
                cols = slice(b * P, (b + 1) * P)
                dve.tensor_tensor(lo[:, :, cols],
                                  psum[:, (BK_T, BK_VT)[b % 2], :].rearrange("p (c t) -> p c t", c=HC),
                                  hi[:, :, cols].bitcast(F32), ALU.subtract).then_inc(ln_lo[k], 1)

            dve.wait_ge(consts_pool, 6)
            dve.tensor_scalar(q_shift[:], part_i[:], NIBBLES - 1, 2, ALU.bitwise_and,
                              ALU.logical_shift_left).then_inc(consts_dve, 1)
            for b in range(NB):
                dve.wait_ge(ld_x[b], 16)
                count(b)
            inverse_deviation(0)
            for b in range(NB):
                if b >= 2:
                    dve.wait_ge(ln_turned[0], b - 1)
                normalise(b, 0)
                if b >= 1:
                    tile_second(b - 1, 0, xt_hi, xt_lo)
            tile_second(NB - 1, 0, xt_hi, xt_lo)

            def v_second(g, n, p):
                dve.wait_ge(vt_hi, g * NH + n + 1)
                dve.tensor_tensor(v_lo[p][:, n * BH:(n + 1) * BH, :],
                                  psum[:, BK_VT, :].rearrange("p (a b) -> p a b", a=BH),
                                  v_hi[p][:, n * BH:(n + 1) * BH, :].bitcast(F32),
                                  ALU.subtract).then_inc(vt_lo, 1)

            v_second(0, 0, 0)
            v_second(0, 1, 0)

            def add_heads(g, u, last):
                dve.wait_ge(o_done, g * NB + u + 1 + PRIME)
                ins = dve.tensor_tensor(xacc[:, u, :], psum[:, BK_O, :], xacc[:, u, :], ALU.add)
                ins.then_inc(o_added, 1)
                if last:
                    dve.wait_ge(o_added, g * NB + u + 1 + PRIME)
                    count(u)

            def group(g, p, more):
                step = g * NB
                for t in range(SLOTS + 1):
                    if t < NB:
                        r = t % 2
                        dve.wait_ge(score_done, step + t + 1 + PRIME)
                        dve.wait_ge(pt_done, step + t - 1 + PRIME)
                        dve.tensor_tensor(probs[:, r], psum[:, BK_S, :].rearrange("p (a b) -> p a b", a=HG),
                                          causal[:].unsqueeze(1).to_broadcast([P, HG, P]),
                                          ALU.add).then_inc(masked, 1)
                        dve.wait_ge(masked, step + t + 1 + PRIME)
                        dve.tensor_reduce(rowmax[:, r, :], probs[:, r], AX_X, ALU.max).then_inc(maxed, 1)
                        dve.wait_ge(maxed, step + t + 1)
                        dve.tensor_scalar(negmax[:, r, :], rowmax[:, r, :], -SCALE, None,
                                          ALU.mult).then_inc(neg_ready, 1)
                    if 1 <= t <= NB:
                        u = t - 1
                        dve.wait_ge(pthi_ready, step + u + 1)
                        dve.tensor_tensor(pt_lo[:], psum[:, BK_T, :].rearrange("p (a b) -> p a b", a=HG),
                                          pt_hi[:].bitcast(F32), ALU.subtract).then_inc(ptlo_ready, 1)
                    if t >= 3:
                        add_heads(g, t - 3, not more)
                    if t < NB:
                        dve.wait_ge(exp_done, step + t + 1)
                        dve.reciprocal(rowinv[:, t % 2, :], rowsum[:, t % 2, :]).then_inc(inv_ready, 1)
                    if more:
                        for i in FILL.get(t, ()):
                            if i in (2, 3):
                                v_second(g + 1, i - 2, 1 - p)
                    if 1 <= t <= NB:
                        u = t - 1
                        dve.wait_ge(athi_ready, step + u + 1)
                        dve.tensor_tensor(at_lo[:, u % 2], psum[:, BK_PV, :].rearrange("p (a b) -> p a b", a=HG),
                                          at_hi[:, u % 2].bitcast(F32), ALU.subtract).then_inc(atlo_ready, 1)

            with dve.Fori(0, NG // 2 - 1) as pair:
                for p in range(2):
                    group(pair * 2 + p, p, True)
            group(NG - 2, 0, True)
            group(NG - 1, 1, False)

            def unpack(m, r, w, loads, unit, group_step, free, down=False):
                dve.wait_ge(ld_f[r], loads)
                if down:
                    q, z = f_q[0:w, r, 0], f_z[0:w, r, 0].rearrange("p a b -> p (a b)")
                    zn, dst = f_zn[0:w].rearrange("p a b -> p (a b)"), f_m[0:w, m]
                    zb = z.unsqueeze(2).to_broadcast([w, H // NIBBLES, NIBBLES])
                    zo = zn.rearrange("p (a b) -> p a b", b=NIBBLES)
                    sh = z_shift[0:w].unsqueeze(1).to_broadcast([w, H // NIBBLES, NIBBLES])
                    zn = f_zn[0:w]
                    rows = w
                else:
                    zw = w // NIBBLES
                    q, z = f_q[:, r, m, :, 0:w], f_z[:, r, m, :, 0:zw]
                    zn, dst = f_zn[:, :, 0:w], f_m[:, m, :, 0:w]
                    zb = z.unsqueeze(3).to_broadcast([P, HC, zw, NIBBLES])
                    zo = zn.rearrange("p c (a b) -> p c a b", b=NIBBLES)
                    sh = z_shift[:].unsqueeze(1).unsqueeze(1).to_broadcast([P, HC, zw, NIBBLES])
                    rows = P
                if free:
                    dve.wait_ge(fm_ready, unit)
                dve.tensor_scalar(q, q, q_shift[0:rows, 0:1], 15, ALU.logical_shift_right,
                                  ALU.bitwise_and).then_inc(fq_step, 1)
                dve.tensor_tensor(zo, zb, sh, ALU.logical_shift_right).then_inc(fq_step, 1)
                dve.wait_ge(fq_step, group_step + 2)
                dve.tensor_scalar(zn, zn, 15, None, ALU.bitwise_and).then_inc(fq_step, 1)
                dve.wait_ge(fq_step, group_step + 3)
                if not isinstance(unit, int) or unit >= 2:
                    dve.wait_ge(fw_ready, unit - 1)
                dve.scalar_tensor_tensor(dst, q, -1.0, zn, ALU.add, ALU.subtract).then_inc(fm_ready, 1)

            TILE_LOADS = 16 * 2 * (HC + 2)
            DOWN_LOADS = 16 * 3
            dve.wait_ge(consts_dve, 1)
            for m in range(2):
                unpack(m, 0, P, TILE_LOADS, m, 3 * m, m > 0)

            inverse_deviation(1)
            for i in range(NB + 2):
                if i < NB:
                    if i >= 2:
                        dve.wait_ge(ln_turned[1], i - 1)
                    normalise(i, 1)
                if 1 <= i <= NB:
                    b = i - 1
                    r = b % 2
                    dve.wait_ge(xs_done, b + 1)
                    dve.tensor_reduce(rowmax[:, r, 0:1], psum[:, (BK_S, BK_PV)[r], 0:P], AX_X,
                                      ALU.max).then_inc(xs_max, 1)
                    dve.wait_ge(xs_max, b + 1)
                    dve.tensor_scalar(negmax[:, r, 0:1], rowmax[:, r, 0:1], -SCALE, None,
                                      ALU.mult).then_inc(xs_neg, 1)
                    dve.wait_ge(xs_exp, b + 1)
                    dve.reciprocal(rowinv[:, r, 0:1], rowsum[:, r, 0:1]).then_inc(xs_inv, 1)
                    dve.wait_ge(xs_inv, b + 1)
                    dve.tensor_scalar(xprobs[:, r, :], xprobs[:, r, :], rowinv[:, r, 0:1], None,
                                      ALU.mult).then_inc(xs_prob, 1)
                if i >= 2:
                    b = i - 2
                    dve.wait_ge(xc_done, b + 1)
                    dve.tensor_tensor(xacc[:, b, :], psum[:, BK_PROJ[b % 2], :], xacc[:, b, :],
                                      ALU.add).then_inc(x_added, 1)
                    dve.wait_ge(x_added, b + 1)
                    count(b)
            inverse_deviation(2)
            for b in range(NB):
                if b >= 2:
                    dve.wait_ge(ln_turned[2], b - 1)
                normalise(b, 2)
                if b >= 1:
                    tile_second(b - 1, 2, ft_hi, ft_lo)
            tile_second(NB - 1, 2, ft_hi, ft_lo)

            def tile_weights(n, r, w, uses):
                for m in range(2):
                    unpack(m, r, w, uses * TILE_LOADS + TILE_LOADS, n * 2 + m, n * 6 + 3 * m, True)

            def down_weights(c):
                r = (NT + c) % 2
                tiles = (NT + 1 - r) // 2
                loads = tiles * TILE_LOADS + (c // 2 + 1) * DOWN_LOADS
                unpack(c % 2, r, width(c), loads, 2 * NT + c, 6 * NT + 3 * c, True, down=True)

            def inner(n, r, w):
                gate = psum[0:w, 4 * r:4 * r + 2, :].rearrange("p a b -> p (a b)")
                up = psum[0:w, 4 * r + 2:4 * r + 4, :].rearrange("p a b -> p (a b)")
                dve.wait_ge(sig_ready, n + 1)
                dve.tensor_tensor(f_sig[0:w, :], gate, f_sig[0:w, :], ALU.mult).then_inc(gs_ready, 1)
                dve.wait_ge(gs_ready, n + 1)
                dve.wait_ge(gu_done, n * 2 + 2 + PRIME)
                dve.wait_ge(intlo_ready, n + PRIME)
                dve.tensor_tensor(f_int[0:w, :], up, f_sig[0:w, :], ALU.mult).then_inc(int_ready, 1)

            with dve.Fori(0, (NT - 3) // 2) as pair:
                for r in range(2):
                    n = pair * 2 + r
                    tile_weights(n + 1, 1 - r, P, pair + r)
                    inner(n, r, P)
            for n in range(NT - 3, NT):
                if n + 1 < NT:
                    tile_weights(n + 1, (n + 1) % 2, width(n + 1), (n + 1) // 2)
                else:
                    down_weights(0)
                inner(n, n % 2, width(n))
            for c in range(1, NT):
                down_weights(c)
            for b in range(NB):
                dve.wait_ge(y16_ready, b + 1)
                dve.tensor_tensor(xacc[:, b, :], xacc[:, b, :], y16[:, b % 2, :], ALU.add).then_inc(y_ready, 1)


_INS = ["x", "ctx_4096", "L0_attn_w_q", "L0_attn_w_k", "L0_attn_w_v", "L0_attn_w_o",
        "L0_ffn_gate_qweight", "L0_ffn_gate_scales", "L0_ffn_gate_zeros",
        "L0_ffn_up_qweight", "L0_ffn_up_scales", "L0_ffn_up_zeros",
        "L0_ffn_down_qweight", "L0_ffn_down_scales", "L0_ffn_down_zeros"]


def kernel(**inputs):
    import numpy as np
    import concourse.bacc as bacc
    from concourse.bass_utils import run_bass_kernel_spmd

    nc = bacc.Bacc("TRN2", target_bir_lowering=False, num_devices=1)
    arrays, args = {}, []
    for name in _INS:
        a = np.ascontiguousarray(inputs[name])
        arrays[f"in_{name}"] = a
        args.append(nc.dram_tensor(f"in_{name}", a.shape, mybir.dt.from_np(a.dtype), kind="ExternalInput").ap())
    shape = inputs["x"].shape
    args.append(nc.dram_tensor("out_0", shape, F32, kind="ExternalOutput").ap())
    decoder_kernel(nc, *args)
    got = run_bass_kernel_spmd(nc, [arrays], core_ids=[0])
    return got.results[0]["out_0"]
```

```python
from contextlib import ExitStack

import concourse.bass as bass
from concourse import mybir

ALU = mybir.AluOpType
ACT = mybir.ActivationFunctionType
AX_X = mybir.AxisListType.X
F32 = mybir.dt.float32
F32R = mybir.dt.float32r
F16 = mybir.dt.float16
I32 = mybir.dt.int32

P = 128
EPS = 1e-5
MASKED = -1e30
NIBBLES = 8
PRIME = 2


def decoder_kernel(nc, x, ctx_in, w_q, w_k, w_v, w_o,
                   gate_q, gate_s, gate_z, up_q, up_s, up_z, down_q, down_s, down_z, out):
    NB, S, H = x.shape
    T = NB * S
    HC = H // P
    NG = w_k.shape[1] // P
    HG = w_q.shape[1] // w_k.shape[1]
    HALF = 512
    NH = T // HALF
    BH = HALF // S
    INTER = gate_q.shape[1]
    NT = (INTER + P - 1) // P
    SCALE = float(P) ** -0.5
    assert S == P and H == HALF and NH == 2 and HG == 4 and NG % 2 == 0

    HBLK = ["k", "v"] + [f"q{j}" for j in range(HG)]
    BLOCKS = [(u, 1) for u in HBLK] + [(u, 0) for u in HBLK]
    NBLK = len(BLOCKS)
    FILL = {0: [0, 1], 1: [2, 3], 2: [4], 3: [5], 4: [6], 5: [7], 6: [8], 7: [9], 8: [10], 9: [11]}
    TURN_V = {1: 1, 6: 0}
    CTX_FILL = {4: [0, 1, 2, 3], 5: [4, 5, 6, 7]}
    SLOTS = NB + 2
    AT_NORM2, AT_SIM, AT_CONTEXT, AT_NORM3, AT_SECOND3 = 4, 5, 6, 7, 8
    ALL_SLOTS = NB + AT_SECOND3
    SPLIT = {0: ["o0", "o1"], 1: ["o2", "o3"], 2: ["k"], 3: ["v"], 4: ["q0"], 5: ["q1"], 6: ["q2"], 7: ["q3"]}
    FIRST_UNITS = len(HBLK)
    UNITS = len(HBLK) + HG

    with ExitStack() as stack:
        def sem(name):
            return stack.enter_context(nc.semaphore(name))

        def allocator(scope):
            return lambda name, shape, dt=F32: scope.enter_context(nc.sbuf_tensor(name, shape, dt))

        sb = allocator(stack)
        xacc = sb("xacc", [P, NB, H])
        xn = sb("xn", [P, 2, H])
        ident = sb("ident", [P, P])
        causal = sb("causal", [P, P])
        stats = sb("stats", [P, NB, 6])
        meanvar = sb("meanvar", [P, NB, 2])
        vareps = sb("vareps", [P, NB])
        shift = sb("shift", [P, NB])
        halfneg = sb("halfneg", [P, 1])
        xm = sb("xm", [P, 2, H])
        f_q = sb("f_q", [P, 2, 2, HC, P], I32)
        f_z = sb("f_z", [P, 2, 2, HC, P // NIBBLES], I32)
        f_s = sb("f_s", [P, 2, 2, HC, P], F16)
        f_zn = sb("f_zn", [P, HC, P], I32)
        f_m = sb("f_m", [P, 2, HC, P])
        f_w = sb("f_w", [P, 2, HC, P])
        rstd = sb("rstd", [P, NB])
        newton = sb("newton", [P, NB])
        rowmax = sb("rowmax", [P, 2, HG])
        negmax = sb("negmax", [P, 2, HG])
        rowsum = sb("rowsum", [P, 2, HG])
        rowinv = sb("rowinv", [P, 2, HG])
        xmax = sb("xmax", [P, 2])
        xneg = sb("xneg", [P, 2])
        xsum = sb("xsum", [P, 2])
        xinv = sb("xinv", [P, 2])
        part_i = sb("part_i", [P, 1], I32)
        q_shift = sb("q_shift", [P, 1], I32)
        z_shift = sb("z_shift", [P, NIBBLES], I32)
        psum = stack.enter_context(nc.psum_tensor("psum", [P, 8, HALF], F32))
        BK_S, BK_T, BK_PV, BK_O, BK_VT, BK_PROJ = 0, 1, 2, 3, 4, (5, 6)
        BK_XT, BK_XS, BK_XC, BK_FT = BK_VT, 7, 5, 6

        with ExitStack() as scope:
            sb = allocator(scope)
            xt_hi = sb("xt_hi", [P, HC, T], F32R)
            xt_lo = sb("xt_lo", [P, HC, T], F32R)
            wq_hi = sb("wq_hi", [P, HG, HC, P], F32R)
            wq_lo = sb("wq_lo", [P, HG, HC, P], F32R)
            wk_hi = sb("wk_hi", [P, HC, P], F32R)
            wk_lo = sb("wk_lo", [P, HC, P], F32R)
            wv_hi = sb("wv_hi", [P, HC, P], F32R)
            wv_lo = sb("wv_lo", [P, HC, P], F32R)
            wq_raw = sb("wq_raw", [P, HC, HG * P])
            wk_raw = sb("wk_raw", [P, HC, P])
            wv_raw = sb("wv_raw", [P, HC, P])
            wo_raw = sb("wo_raw", [P, HG, H])
            wo_hi = sb("wo_hi", [P, HG, H], F32R)
            wo_lo = sb("wo_lo", [P, HG, H], F32R)
            qt = sb("qt", [P, HG, T])
            kt = sb("kt", [P, T])
            vt = sb("vt", [P, HALF])
            v_hi = sb("v_hi", [P, NB, P], F32R)
            v_lo = sb("v_lo", [P, NB, P], F32R)
            probs = sb("probs", [P, 2, HG, P])
            pt_hi = sb("pt_hi", [P, HG, P], F32R)
            pt_lo = sb("pt_lo", [P, HG, P], F32R)
            at_hi = sb("at_hi", [P, 2, HG, P], F32R)
            at_lo = sb("at_lo", [P, 2, HG, P], F32R)
        with ExitStack() as scope:
            sb = allocator(scope)
            cx = sb("cx", [P, NB, H])
            cxt = sb("cxt", [P, HC, T])
            query_t = sb("query_t", [P, 2, HC, P])
            xprobs = sb("xprobs", [P, 2, P])
        with ExitStack() as scope:
            sb = allocator(scope)
            int_hi = sb("int_hi", [P, NT, T], F32R)
            ft_hi = sb("ft_hi", [P, HC, T], F32R)
            ft_lo = sb("ft_lo", [P, HC, T], F32R)
            int_lo = sb("int_lo", [P, NT, T], F32R)
            f_hi = sb("f_hi", [P, 2, 2, HC, P], F32R)
            f_lo = sb("f_lo", [P, 2, 2, HC, P], F32R)
            f_sig = sb("f_sig", [P, T])
            f_int = sb("f_int", [P, T])
            y16 = sb("y16", [P, 2, H], F16)

        ld_x = [sem(f"ld_x{b}") for b in range(NB)]
        ld_w = {k: sem(f"ld_w{k}") for k in "qkvo"}
        ld_cx = sem("ld_cx")
        consts_pool = sem("consts_pool")
        consts_dve = sem("consts_dve")
        stat_step = sem("stat_step")
        var_ready = [sem(f"var_ready{i}") for i in range(3)]
        rstd_step = sem("rstd_step")
        rstd_ready = [sem(f"rstd_ready{i}") for i in range(3)]
        ln_ready = [sem(f"ln_ready{i}") for i in range(3)]
        ln_turned = [sem(f"ln_turned{i}") for i in range(3)]
        ln_hi = [sem(f"ln_hi{i}") for i in range(3)]
        ln_lo = [sem(f"ln_lo{i}") for i in range(3)]
        w_hi = sem("w_hi")
        w_lo = sem("w_lo")
        proj_done = sem("proj_done")
        proj_out = sem("proj_out")
        vt_done = sem("vt_done")
        vt_hi = sem("vt_hi")
        vt_lo = sem("vt_lo")
        score_done = sem("score_done")
        masked = sem("masked")
        maxed = sem("maxed")
        neg_ready = sem("neg_ready")
        exp_done = sem("exp_done")
        inv_ready = sem("inv_ready")
        prob_ready = sem("prob_ready")
        pt_done = sem("pt_done")
        pthi_ready = sem("pthi_ready")
        ptlo_ready = sem("ptlo_ready")
        pv_done = sem("pv_done")
        athi_ready = sem("athi_ready")
        atlo_ready = sem("atlo_ready")
        o_done = sem("o_done")
        o_added = sem("o_added")
        xs_done = sem("xs_done")
        xs_max = sem("xs_max")
        xs_neg = sem("xs_neg")
        xs_exp = sem("xs_exp")
        xs_inv = sem("xs_inv")
        xs_prob = sem("xs_prob")
        xc_done = sem("xc_done")
        x_added = sem("x_added")
        ld_f = [sem(f"ld_f{i}") for i in range(2)]
        fq_step = sem("fq_step")
        fm_ready = sem("fm_ready")
        fw_ready = sem("fw_ready")
        fhi_ready = sem("fhi_ready")
        flo_ready = sem("flo_ready")
        gu_done = sem("gu_done")
        sig_ready = sem("sig_ready")
        gs_ready = sem("gs_ready")
        int_ready = sem("int_ready")
        inthi_ready = sem("inthi_ready")
        intlo_ready = sem("intlo_ready")
        down_done = sem("down_done")
        y16_ready = sem("y16_ready")
        y_ready = sem("y_ready")
        stored = sem("stored")

        FIRST_BLOCKS = len(HBLK)
        CTX_BLOCKS = NG * NBLK
        LAST = NG - 1
        ATT = NG * NB
        TILES = NB

        def weight(unit, raw=False):
            kind, j = unit[0], int(unit[1:] or 0)
            if raw:
                return {"k": lambda: wk_raw[:], "v": lambda: wv_raw[:],
                        "q": lambda: wq_raw[:, :, j * P:(j + 1) * P], "o": lambda: wo_raw[:, j]}[kind]()
            return {"k": lambda: (wk_hi[:], wk_lo[:]), "v": lambda: (wv_hi[:], wv_lo[:]),
                    "q": lambda: (wq_hi[:, j], wq_lo[:, j]), "o": lambda: (wo_hi[:, j], wo_lo[:, j])}[kind]()

        def width(n):
            return min(P, INTER - n * P)

        block = stack.enter_context(nc.Block())

        @block.sync
        def _(sp):
            wq_v = w_q.rearrange("(c p) n -> p c n", p=P)
            wk_v = w_k.rearrange("(c p) n -> p c n", p=P)
            wv_v = w_v.rearrange("(c p) n -> p c n", p=P)
            wo_v = w_o.rearrange("(h p) n -> p h n", p=P)

            def load_w(kind, g):
                dst, src = {
                    "q": (wq_raw, lambda: wq_v[:, :, g * HG * P:(g + 1) * HG * P]),
                    "k": (wk_raw, lambda: wk_v[:, :, g * P:(g + 1) * P]),
                    "v": (wv_raw, lambda: wv_v[:, :, g * P:(g + 1) * P]),
                    "o": (wo_raw, lambda: wo_v[:, g * HG:(g + 1) * HG, :]),
                }[kind]
                sp.dma_start(dst[:], src()).then_inc(ld_w[kind], 16)

            def load_ffn(n):
                r, c0, w = n % 2, n * P, width(n)
                for m, (q, s, z) in enumerate(((gate_q, gate_s, gate_z), (up_q, up_s, up_z))):
                    for c in range(HC):
                        rows = q[c * P // NIBBLES:(c + 1) * P // NIBBLES, c0:c0 + w]
                        sp.dma_start(f_q[:, r, m, c, 0:w],
                                     rows.unsqueeze(1).to_broadcast([P // NIBBLES, NIBBLES, w])
                                     ).then_inc(ld_f[r], 16)
                    sp.dma_start(f_s[:, r, m, :, 0:w],
                                 s[:, c0:c0 + w].unsqueeze(0).to_broadcast([P, HC, w])).then_inc(ld_f[r], 16)
                    zc, zw = c0 // NIBBLES, w // NIBBLES
                    sp.dma_start(f_z[:, r, m, :, 0:zw],
                                 z[:, zc:zc + zw].unsqueeze(0).to_broadcast([P, HC, zw])).then_inc(ld_f[r], 16)

            def load_down(c):
                r, w = (NT + c) % 2, width(c)
                rows = down_q[c * P // NIBBLES:(c * P + w) // NIBBLES, :]
                sp.dma_start(f_q[0:w, r, 0].rearrange("p a b -> p (a b)"),
                             rows.unsqueeze(1).to_broadcast([w // NIBBLES, NIBBLES, H])).then_inc(ld_f[r], 16)
                sp.dma_start(f_s[0:w, r, 0].rearrange("p a b -> p (a b)"),
                             down_s[c:c + 1, :].to_broadcast([w, H])).then_inc(ld_f[r], 16)
                sp.dma_start(f_z[0:w, r, 0].rearrange("p a b -> p (a b)"),
                             down_z[c:c + 1, :].to_broadcast([w, H // NIBBLES])).then_inc(ld_f[r], 16)

            for b in range(NB):
                sp.dma_start(xacc[:, b, :], x[b]).then_inc(ld_x[b], 16)
                if b == BH - 1:
                    load_w("k", 0)
                    load_w("v", 0)
                    load_w("q", 0)
            load_w("o", 0)
            load_ffn(0)
            load_ffn(1)
            for g in range(NG):
                before = g * UNITS + (0 if g == 0 else HG)
                if g + 1 < NG:
                    sp.wait_ge(w_lo, before + 1)
                    load_w("k", g + 1)
                    sp.wait_ge(w_lo, before + 2)
                    load_w("v", g + 1)
                    sp.wait_ge(w_lo, before + 2 + HG)
                    load_w("q", g + 1)
                    sp.wait_ge(w_lo, g * UNITS + FIRST_UNITS + HG)
                    load_w("o", g + 1)
            sp.wait_ge(proj_done, CTX_BLOCKS)
            sp.dma_start(cx[:], ctx_in.rearrange("b c s -> c b s")).then_inc(ld_cx, 16)

            for n in range(2, NT):
                sp.wait_ge(fm_ready, 2 * (n - 1))
                sp.wait_ge(fw_ready, 2 * (n - 1))
                load_ffn(n)
            for c in range(NT):
                done = 2 * (NT - 1) if c == 0 else 2 * NT + c - 1
                sp.wait_ge(fm_ready, done)
                sp.wait_ge(fw_ready, done)
                load_down(c)
            for b in range(NB):
                sp.wait_ge(y_ready, b + 1)
                sp.dma_start(out[b], xacc[:, b, :]).then_inc(stored, 16)
            sp.wait_ge(stored, 16 * NB)

        @block.tensor
        def _(pe):
            for s in (score_done, pt_done, pv_done, o_done, gu_done):
                pe.sem_inc(s, PRIME)

            def passes(dst, a_hi, a_lo, b_hi, b_lo, start, stop):
                pe.matmul(dst, a_hi, b_hi, start=start, stop=False)
                pe.matmul(dst, a_hi, b_lo, start=False, stop=False)
                return pe.matmul(dst, a_lo, b_hi, start=False, stop=stop)

            def turn_tile(bank, src):
                for c in range(HC):
                    mm = pe.transpose(psum[:, bank, c * P:(c + 1) * P], src[:, c * P:(c + 1) * P], ident[:])
                return mm

            def project(unit, n, bank):
                hi, lo = weight(unit)
                cols = slice(n * HALF, (n + 1) * HALF)
                for c in range(HC):
                    mm = passes(psum[:, bank, :], hi[:, c, :], lo[:, c, :], xt_hi[:, c, cols],
                                xt_lo[:, c, cols], c == 0, c == HC - 1)
                mm.then_inc(proj_done, 1)

            def turn_v():
                for k in range(BH):
                    mm = pe.transpose(psum[:, BK_VT, k * P:(k + 1) * P], vt[:, k * P:(k + 1) * P], ident[:])
                mm.then_inc(vt_done, 1)

            pe.wait_ge(consts_pool, 4)
            for b in range(NB):
                pe.wait_ge(ln_ready[0], b + 1)
                if b >= 2:
                    pe.wait_ge(ln_lo[0], b - 1)
                turn_tile((BK_T, BK_VT)[b % 2], xn[:, b % 2, :]).then_inc(ln_turned[0], 1)
                if b >= BH:
                    i = b - BH
                    pe.wait_ge(ln_lo[0], max(BH, b - 1))
                    pe.wait_ge(w_lo, i + 1)
                    if i >= 2:
                        pe.wait_ge(proj_out, i - 1)
                    project(HBLK[i], 0, BK_PROJ[i % 2])
            pe.wait_ge(ln_lo[0], NB)
            pe.wait_ge(proj_out, 2)
            turn_v()
            for i in range(NB - BH, FIRST_BLOCKS):
                pe.wait_ge(w_lo, i + 1)
                pe.wait_ge(proj_out, i - 1)
                project(HBLK[i], 0, BK_PROJ[i % 2])

            def cross_first(t):
                for b in CTX_FILL.get(t, ()):
                    if b == 0:
                        pe.wait_ge(ld_cx, 16)
                    pe.wait_ge(proj_out, CTX_BLOCKS + b - 1)
                    turn_tile(BK_PROJ[b % 2], cx[:, b, :]).then_inc(proj_done, 1)
                b = t - AT_SIM
                if 0 <= b < NB:
                    pe.wait_ge(ln_hi[1], b + 1)
                    pe.wait_ge(proj_out, CTX_BLOCKS + b + 1)
                    if b >= 1:
                        pe.wait_ge(xs_exp, b)
                    for c in range(HC):
                        mm = pe.matmul(psum[:, BK_XS, 0:P], query_t[:, b % 2, c, :],
                                       cxt[:, c, b * P:(b + 1) * P], start=(c == 0), stop=(c == HC - 1))
                    mm.then_inc(xs_done, 1)
                b = t - AT_NORM2
                if 0 <= b < NB:
                    pe.wait_ge(ln_ready[1], b + 1)
                    if b >= 1:
                        pe.wait_ge(ln_hi[1], b)
                    turn_tile(BK_XT, xn[:, b % 2, :]).then_inc(ln_turned[1], 1)

            def cross_second(t):
                b = t - AT_CONTEXT
                if 0 <= b < NB:
                    pe.wait_ge(xs_prob, b + 1)
                    if b == 0:
                        pe.wait_ge(proj_out, CTX_BLOCKS + NB)
                    else:
                        pe.wait_ge(x_added, b)
                    pe.matmul(psum[:, BK_XC, :], xprobs[:, b % 2, :], cx[:, b, :],
                              start=True, stop=True).then_inc(xc_done, 1)
                b = t - AT_NORM3
                if 0 <= b < NB:
                    pe.wait_ge(ln_ready[2], b + 1)
                    if b >= 1:
                        pe.wait_ge(ln_lo[2], b)
                    turn_tile(BK_FT, xm[:, b % 2, :]).then_inc(ln_turned[2], 1)

            def group(g, more):
                step, blocks = g * NB, g * NBLK + FIRST_BLOCKS
                for t in range(SLOTS):
                    if t < NB:
                        pe.wait_ge(masked, step + t + PRIME)
                        pe.wait_ge(proj_out, blocks + (0 if t < BH else len(HBLK)))
                        for j in range(HG):
                            mm = pe.matmul(psum[:, BK_S, j * P:(j + 1) * P],
                                           qt[:, j, t * P:(t + 1) * P], kt[:, t * P:(t + 1) * P],
                                           start=True, stop=True)
                        mm.then_inc(score_done, 1)
                    if 1 <= t <= NB:
                        u = t - 1
                        pe.wait_ge(prob_ready, step + u + 1)
                        pe.wait_ge(ptlo_ready, step + u + PRIME)
                        for j in range(HG):
                            mm = pe.transpose(psum[:, BK_T, j * P:(j + 1) * P], probs[:, u % 2, j, :], ident[:])
                        mm.then_inc(pt_done, 1)
                    if t in TURN_V and (more or TURN_V[t] == 1):
                        n = TURN_V[t]
                        i = BLOCKS.index(("v", n))
                        pe.wait_ge(proj_out, blocks + i + 1)
                        pe.wait_ge(vt_lo, g * NH + (2 - n))
                        turn_v()
                    for i in FILL[t]:
                        unit, n = BLOCKS[i]
                        if n == 0 and not more:
                            continue
                        k = HBLK.index(unit)
                        pe.wait_ge(w_lo, g * UNITS + (k + 1 if n == 1 else FIRST_UNITS + HG + k + 1))
                        pe.wait_ge(proj_out, blocks + i - 1)
                        project(unit, n, BK_PROJ[i % 2])
                    if not more:
                        cross_first(t)
                    if 1 <= t <= NB:
                        u = t - 1
                        pe.wait_ge(ptlo_ready, step + u + 1 + PRIME)
                        pe.wait_ge(vt_lo, g * NH + (1 if u < BH else 2))
                        pe.wait_ge(atlo_ready, step + u + PRIME)
                        passes(psum[:, BK_PV, :], v_hi[:, u, :], v_lo[:, u, :],
                               pt_hi[:].rearrange("p a b -> p (a b)"), pt_lo[:].rearrange("p a b -> p (a b)"),
                               True, True).then_inc(pv_done, 1)
                    if not more:
                        cross_second(t)
                    if t >= 2:
                        u = t - 2
                        pe.wait_ge(atlo_ready, step + u + 1 + PRIME)
                        pe.wait_ge(w_lo, g * UNITS + FIRST_UNITS + HG)
                        pe.wait_ge(o_added, step + u + PRIME)
                        for j in range(HG):
                            mm = passes(psum[:, BK_O, :], at_hi[:, u % 2, j, :], at_lo[:, u % 2, j, :],
                                        wo_hi[:, j, :], wo_lo[:, j, :], j == 0, j == HG - 1)
                        mm.then_inc(o_done, 1)

            with pe.Fori(0, LAST) as g:
                group(g, True)
            group(LAST, False)

            for t in range(SLOTS, ALL_SLOTS):
                cross_first(t)
                cross_second(t)
            pe.wait_ge(ln_lo[2], NB)

            def gate_up(n, r, w):
                for m in range(2):
                    pe.wait_ge(flo_ready, n * 2 + m + 1)
                    if m == 0:
                        pe.wait_ge(int_ready, n + PRIME - 1)
                    for h in range(NH):
                        for c in range(HC):
                            cols = slice(h * HALF, (h + 1) * HALF)
                            mm = passes(psum[0:w, 4 * r + 2 * m + h, :], f_hi[:, r, m, c, 0:w],
                                        f_lo[:, r, m, c, 0:w], ft_hi[:, c, cols], ft_lo[:, c, cols],
                                        c == 0, c == HC - 1)
                    mm.then_inc(gu_done, 1)

            with pe.Fori(0, (NT - 3) // 2) as pair:
                for r in range(2):
                    gate_up(pair * 2 + r, r, P)
            for n in range(NT - 3, NT):
                gate_up(n, n % 2, width(n))

            for c in range(NT):
                w, r, m = width(c), (NT + c) % 2, (c // 2) % 2
                pe.wait_ge(flo_ready, 2 * NT + c + 1)
                pe.wait_ge(intlo_ready, c + 1 + PRIME)
                for k in range(NB):
                    b = (k + BH) % NB if c == 0 else k
                    if c == 0 and k == 0:
                        pe.wait_ge(int_ready, NT - 1 + PRIME)
                    if c == 0 and b == 0:
                        pe.wait_ge(int_ready, NT + PRIME)
                    mm = passes(psum[:, b, :], int_hi[0:w, c, b * P:(b + 1) * P], int_lo[0:w, c, b * P:(b + 1) * P],
                                f_hi[0:w, r, m].rearrange("p a b -> p (a b)"),
                                f_lo[0:w, r, m].rearrange("p a b -> p (a b)"), c == 0, c == NT - 1)
                    if c == NT - 1:
                        mm.then_inc(down_done, 1)
                if c < NT - 1:
                    mm.then_inc(gu_done, 1)

        @block.scalar
        def _(act):
            def split_first(unit):
                act.copy(weight(unit)[0], weight(unit, raw=True)).then_inc(w_hi, 1)

            def tile_first(b, k, hi, bank):
                act.wait_ge(ln_turned[k], b + 1)
                act.copy(hi[:, :, b * P:(b + 1) * P],
                         psum[:, bank, :].rearrange("p (c t) -> p c t", c=HC)).then_inc(ln_hi[k], 1)

            def project_out(unit, n, bank):
                cols = slice(n * HALF, (n + 1) * HALF)
                dst = vt[:] if unit == "v" else kt[:, cols] if unit == "k" else qt[:, int(unit[1:]), cols]
                act.copy(dst, psum[:, bank, :]).then_inc(proj_out, 1)

            def v_first(n):
                act.copy(v_hi[:, n * BH:(n + 1) * BH, :],
                         psum[:, BK_VT, :].rearrange("p (a b) -> p a b", a=BH)).then_inc(vt_hi, 1)

            def first_unit(i):
                act.wait_ge(ld_w[HBLK[i][0]], 16)
                split_first(HBLK[i])

            def normalise(b, k, dst):
                act.wait_ge(rstd_ready[k], b + 1)
                if b >= 2:
                    act.wait_ge(ln_turned[k], b - 1)
                act.activation(dst[:, b % 2, :], xacc[:, b, :], ACT.Identity, bias=shift[:, b:b + 1],
                               scale=rstd[:, b:b + 1]).then_inc(ln_ready[k], 1)

            for i in range(NB + 1):
                if i < NB:
                    normalise(i, 0, xn)
                if i >= 1:
                    tile_first(i - 1, 0, xt_hi, (BK_T, BK_VT)[(i - 1) % 2])
                if 1 <= i <= FIRST_UNITS:
                    first_unit(i - 1)
                if i >= BH + 2:
                    j = i - BH - 2
                    act.wait_ge(proj_done, j + 1)
                    project_out(HBLK[j], 0, BK_PROJ[j % 2])
            for i in range(NB - BH - 1, FIRST_BLOCKS):
                if i == 3:
                    act.wait_ge(vt_done, 1)
                    v_first(0)
                act.wait_ge(proj_done, i + 1)
                project_out(HBLK[i], 0, BK_PROJ[i % 2])

            def cross_first(t):
                b = t - AT_NORM2
                if 0 <= b < NB:
                    normalise(b, 1, xn)
                for b in CTX_FILL.get(t, ()):
                    act.wait_ge(proj_done, CTX_BLOCKS + b + 1)
                    act.copy(cxt[:, :, b * P:(b + 1) * P],
                             psum[:, BK_PROJ[b % 2], :].rearrange("p (c t) -> p c t", c=HC)
                             ).then_inc(proj_out, 1)
                b = t - AT_SIM
                if 0 <= b < NB:
                    act.wait_ge(xs_neg, b + 1)
                    if b >= 2:
                        act.wait_ge(xc_done, b - 1)
                    act.activation(xprobs[:, b % 2, :], psum[:, BK_XS, 0:P], ACT.Exp,
                                   bias=xneg[:, b % 2:b % 2 + 1], scale=SCALE,
                                   accum_out=xsum[:, b % 2:b % 2 + 1]).then_inc(xs_exp, 1)
                b = t - AT_NORM2
                if 0 <= b < NB:
                    act.wait_ge(ln_turned[1], b + 1)
                    if b >= 2:
                        act.wait_ge(xs_done, b - 1)
                    act.copy(query_t[:, b % 2], psum[:, BK_XT, :].rearrange("p (c t) -> p c t", c=HC)
                             ).then_inc(ln_hi[1], 1)

            def cross_second(t):
                b = t - AT_NORM3
                if 0 <= b < NB:
                    normalise(b, 2, xm)
                    tile_first(b, 2, ft_hi, BK_FT)

            def group(g, more):
                step, blocks = g * NB, g * NBLK + FIRST_BLOCKS
                for t in range(SLOTS):
                    if 1 <= t <= NB:
                        u = t - 1
                        act.wait_ge(pt_done, step + u + 1 + PRIME)
                        act.wait_ge(pv_done, step + u + PRIME)
                        act.copy(pt_hi[:], psum[:, BK_T, :].rearrange("p (a b) -> p a b", a=HG)
                                 ).then_inc(pthi_ready, 1)
                    if t < NB:
                        act.wait_ge(neg_ready, step + t + 1)
                        for j in range(HG):
                            e = act.activation(probs[:, t % 2, j, :], probs[:, t % 2, j, :], ACT.Exp,
                                               bias=negmax[:, t % 2, j:j + 1], scale=SCALE,
                                               accum_out=rowsum[:, t % 2, j:j + 1])
                        e.then_inc(exp_done, 1)
                    if t in TURN_V and (more or TURN_V[t] == 1):
                        n = TURN_V[t]
                        act.wait_ge(vt_done, g * NH + (3 - n))
                        act.wait_ge(pv_done, step + (0 if n == 1 else BH) + PRIME)
                        v_first(n)
                    for i in FILL[t]:
                        unit, n = BLOCKS[i]
                        if n == 0 and not more:
                            continue
                        act.wait_ge(proj_done, blocks + i + 1)
                        if unit == "v":
                            act.wait_ge(vt_done, g * NH + (2 - n))
                        else:
                            act.wait_ge(score_done, step + (0 if n == 1 else BH) + PRIME)
                        project_out(unit, n, BK_PROJ[i % 2])
                    if not more:
                        cross_first(t)
                    if 1 <= t <= NB:
                        u = t - 1
                        act.wait_ge(pv_done, step + u + 1 + PRIME)
                        act.wait_ge(o_done, step + u - 1 + PRIME)
                        act.copy(at_hi[:, u % 2], psum[:, BK_PV, :].rearrange("p (a b) -> p a b", a=HG)
                                 ).then_inc(athi_ready, 1)
                    if not more:
                        cross_second(t)
                    for unit in SPLIT.get(t, ()):
                        if unit[0] == "o":
                            if unit == "o0":
                                act.wait_ge(ld_w["o"], g * 16 + 16)
                                act.wait_ge(o_done, step + PRIME)
                            split_first(unit)
                        elif more:
                            act.wait_ge(ld_w[unit[0]], g * 16 + 32)
                            act.wait_ge(proj_done, blocks + BLOCKS.index((unit, 1)) + 1)
                            split_first(unit)

            with act.Fori(0, LAST) as g:
                group(g, True)
            group(LAST, False)

            for t in range(SLOTS, ALL_SLOTS):
                cross_first(t)
                cross_second(t)
                if t == SLOTS:
                    act.wait_ge(o_done, ATT + PRIME)
                    for m in range(2):
                        act.wait_ge(fw_ready, m + 1)
                        act.copy(f_hi[:, 0, m], f_w[:, m]).then_inc(fhi_ready, 1)

            def weight_first(unit, r, m, before, w):
                act.wait_ge(fw_ready, unit + 1)
                act.wait_ge(gu_done, before + PRIME)
                act.copy(f_hi[:, r, m, :, 0:w], f_w[:, m, :, 0:w]).then_inc(fhi_ready, 1)

            def tile_weights(n, r, w):
                for m in range(2):
                    weight_first(n * 2 + m, r, m, n * 2 + m - 3, w)

            def down_weights(c):
                w, r, m = width(c), (NT + c) % 2, (c // 2) % 2
                act.wait_ge(fw_ready, 2 * NT + c + 1)
                act.wait_ge(gu_done, (2 * (NT - 2 + c % 2) + m + 1 if c < 4 else 2 * NT + c - 3) + PRIME)
                act.copy(f_hi[0:w, r, m], f_w[0:w, c % 2]).then_inc(fhi_ready, 1)

            def inner(n, r, w):
                act.wait_ge(gu_done, n * 2 + 1 + PRIME)
                act.wait_ge(int_ready, n + PRIME)
                gate = psum[0:w, 4 * r:4 * r + 2, :].rearrange("p a b -> p (a b)")
                act.activation(f_sig[0:w, :], gate, ACT.Sigmoid).then_inc(sig_ready, 1)

            def inner_first(n, w):
                act.wait_ge(int_ready, n + 1 + PRIME)
                act.copy(int_hi[0:w, bass.ds(n, 1), :].rearrange("p a b -> p (a b)"),
                         f_int[0:w, :]).then_inc(inthi_ready, 1)

            with act.Fori(0, (NT - 3) // 2) as pair:
                for r in range(2):
                    n = pair * 2 + r
                    inner(n, r, P)
                    tile_weights(n + 1, 1 - r, P)
                    inner_first(n, P)
            for n in range(NT - 3, NT):
                inner(n, n % 2, width(n))
                if n + 1 < NT:
                    tile_weights(n + 1, (n + 1) % 2, width(n + 1))
                else:
                    down_weights(0)
                inner_first(n, width(n))
            for c in range(1, NT):
                down_weights(c)
            for b in range(NB):
                act.wait_ge(down_done, b + 1)
                if b >= 2:
                    act.wait_ge(y_ready, b - 1)
                act.copy(y16[:, b % 2, :], psum[:, b, :]).then_inc(y16_ready, 1)

        @block.gpsimd
        def _(pool):
            pool.memset(ident[:], 0.0).then_inc(consts_pool, 1)
            pool.memset(causal[:], 0.0).then_inc(consts_pool, 1)
            pool.wait_ge(consts_pool, 2)
            pool.affine_select(out=ident[:], in_=ident[:], compare_op=ALU.not_equal, fill=1.0,
                               base=0, pattern=[[-1, P]], channel_multiplier=1).then_inc(consts_pool, 1)
            pool.affine_select(out=causal[:], in_=causal[:], compare_op=ALU.is_ge, fill=MASKED,
                               base=0, pattern=[[-1, P]], channel_multiplier=1).then_inc(consts_pool, 1)
            pool.iota(part_i[:], pattern=[[0, 1]], base=0, channel_multiplier=1).then_inc(consts_pool, 1)
            pool.iota(z_shift[:], pattern=[[4, NIBBLES]], base=0, channel_multiplier=0).then_inc(consts_pool, 1)
            pool.sem_inc(intlo_ready, PRIME)

            pool.memset(halfneg[:], -0.5).then_inc(consts_pool, 1)
            pool.wait_ge(consts_pool, 7)
            steps = [0]

            def after(ins):
                steps[0] += 1
                ins.then_inc(rstd_step, 1)
                pool.wait_ge(rstd_step, steps[0])

            def inverse_deviation(b, k):
                v, r, n = vareps[:, b:b + 1], rstd[:, b:b + 1], newton[:, b:b + 1]
                pool.wait_ge(var_ready[k], b + 1)
                after(pool.tensor_scalar(v, meanvar[:, b, 1:2], EPS, 1.0, ALU.add, ALU.mult))
                after(pool.tensor_tensor(r, v, halfneg[:], ALU.pow))
                after(pool.tensor_tensor(n, r, r, ALU.mult))
                after(pool.tensor_tensor(n, n, v, ALU.mult))
                after(pool.tensor_scalar(n, n, -0.5, 1.5, ALU.mult, ALU.add))
                after(pool.tensor_tensor(r, r, n, ALU.mult))
                pool.tensor_scalar(shift[:, b:b + 1], meanvar[:, b, 0:1], r, -1.0, ALU.mult,
                                   ALU.mult).then_inc(rstd_ready[k], 1)

            def split_second(unit, count):
                hi, lo = weight(unit)
                pool.wait_ge(w_hi, count)
                pool.tensor_tensor(lo, weight(unit, raw=True), hi.bitcast(F32), ALU.subtract).then_inc(w_lo, 1)

            for b in range(NB):
                inverse_deviation(b, 0)
                if b >= BH:
                    split_second(HBLK[b - BH], b - BH + 1)
            for i in range(NB - BH, FIRST_UNITS):
                split_second(HBLK[i], i + 1)

            def group(g, more):
                step, n = g * NB, 0
                for t in range(SLOTS):
                    if t < NB:
                        pool.wait_ge(inv_ready, step + t + 1)
                        pool.tensor_tensor(probs[:, t % 2], probs[:, t % 2],
                                           rowinv[:, t % 2, :].unsqueeze(2).to_broadcast([P, HG, P]),
                                           ALU.mult).then_inc(prob_ready, 1)
                    for unit in SPLIT.get(t, ()):
                        if unit[0] == "o" or more:
                            n += 1
                            split_second(unit, g * UNITS + FIRST_UNITS + n)
                    if not more and t == 3:
                        scaled(0, 0, 0, P)
                        scaled(1, 1, 0, P)
                    if not more:
                        cross(t)

            def cross(t):
                b = t - AT_NORM2 + 1
                if 0 <= b < NB:
                    inverse_deviation(b, 1)
                b = t - AT_CONTEXT
                if 0 <= b < NB:
                    inverse_deviation(b, 2)

            def scaled(unit, m, r, w):
                pool.wait_ge(fm_ready, unit + 1)
                pool.tensor_tensor(f_w[:, m, :, 0:w], f_m[:, m, :, 0:w], f_s[:, r, m, :, 0:w],
                                   ALU.mult).then_inc(fw_ready, 1)

            def second(unit, m, r, w):
                pool.wait_ge(fhi_ready, unit + 1)
                pool.tensor_tensor(f_lo[:, r, m, :, 0:w], f_w[:, m, :, 0:w],
                                   f_hi[:, r, m, :, 0:w].bitcast(F32), ALU.subtract).then_inc(flo_ready, 1)

            with pool.Fori(0, LAST) as g:
                group(g, True)
            group(LAST, False)
            for t in range(SLOTS, ALL_SLOTS):
                cross(t)
                if t == SLOTS:
                    pool.wait_ge(o_done, ATT + PRIME)
                    second(0, 0, 0, P)
                    second(1, 1, 0, P)

            def tile_weights(n, r, w):
                for m in range(2):
                    pool.wait_ge(flo_ready, n * 2 + m - 1)
                    scaled(n * 2 + m, m, r, w)
                for m in range(2):
                    second(n * 2 + m, m, r, w)

            def down_weights(c):
                w, r, unit, m = width(c), (NT + c) % 2, 2 * NT + c, c % 2
                pool.wait_ge(fm_ready, unit + 1)
                pool.wait_ge(flo_ready, unit - 1)
                pool.tensor_tensor(f_w[0:w, m], f_m[0:w, m], f_s[0:w, r, 0], ALU.mult).then_inc(fw_ready, 1)
                pool.wait_ge(fhi_ready, unit + 1)
                k = (c // 2) % 2
                pool.tensor_tensor(f_lo[0:w, r, k], f_w[0:w, m], f_hi[0:w, r, k].bitcast(F32),
                                   ALU.subtract).then_inc(flo_ready, 1)

            def inner_second(n, w):
                pool.wait_ge(inthi_ready, n + 1)
                at = bass.ds(n, 1)
                pool.tensor_tensor(int_lo[0:w, at, :].rearrange("p a b -> p (a b)"), f_int[0:w, :],
                                   int_hi[0:w, at, :].rearrange("p a b -> p (a b)").bitcast(F32),
                                   ALU.subtract).then_inc(intlo_ready, 1)

            with pool.Fori(0, (NT - 3) // 2) as pair:
                for r in range(2):
                    n = pair * 2 + r
                    tile_weights(n + 1, 1 - r, P)
                    inner_second(n, P)
            for n in range(NT - 3, NT):
                if n + 1 < NT:
                    tile_weights(n + 1, (n + 1) % 2, width(n + 1))
                else:
                    down_weights(0)
                inner_second(n, width(n))
            for c in range(1, NT):
                down_weights(c)

        @block.vector
        def _(dve):
            for s in (masked, ptlo_ready, atlo_ready, o_added, int_ready):
                dve.sem_inc(s, PRIME)
            steps = [0]

            def after(ins):
                steps[0] += 1
                ins.then_inc(stat_step, 1)
                dve.wait_ge(stat_step, steps[0])

            def count(b, k):
                after(dve.bn_stats(stats[:, b, :], xacc[:, b, :]))
                dve.bn_aggr(meanvar[:, b, :], stats[:, b, :]).then_inc(var_ready[k], 1)

            def tile_second(b, k, hi, lo, bank):
                dve.wait_ge(ln_hi[k], b + 1)
                cols = slice(b * P, (b + 1) * P)
                dve.tensor_tensor(lo[:, :, cols], psum[:, bank, :].rearrange("p (c t) -> p c t", c=HC),
                                  hi[:, :, cols].bitcast(F32), ALU.subtract).then_inc(ln_lo[k], 1)

            for i in range(NB + 2):
                if i < NB:
                    dve.wait_ge(ld_x[i], 16)
                    count(i, 0)
                if i >= 2:
                    tile_second(i - 2, 0, xt_hi, xt_lo, (BK_T, BK_VT)[i % 2])
            dve.wait_ge(consts_pool, 7)
            dve.tensor_scalar(q_shift[:], part_i[:], NIBBLES - 1, 2, ALU.bitwise_and,
                              ALU.logical_shift_left).then_inc(consts_dve, 1)

            def v_second(n):
                dve.tensor_tensor(v_lo[:, n * BH:(n + 1) * BH, :],
                                  psum[:, BK_VT, :].rearrange("p (a b) -> p a b", a=BH),
                                  v_hi[:, n * BH:(n + 1) * BH, :].bitcast(F32),
                                  ALU.subtract).then_inc(vt_lo, 1)

            dve.wait_ge(vt_hi, 1)
            v_second(0)

            def cross_max(t):
                b = t - AT_SIM
                if 0 <= b < NB:
                    r = slice(b % 2, b % 2 + 1)
                    dve.wait_ge(xs_done, b + 1)
                    dve.tensor_reduce(xmax[:, r], psum[:, BK_XS, 0:P], AX_X, ALU.max).then_inc(xs_max, 1)
                    dve.wait_ge(xs_max, b + 1)
                    dve.tensor_scalar(xneg[:, r], xmax[:, r], -SCALE, None, ALU.mult).then_inc(xs_neg, 1)
                b = t - AT_SECOND3
                if 0 <= b < NB:
                    tile_second(b, 2, ft_hi, ft_lo, BK_FT)

            def cross_inverse(t):
                b = t - AT_SIM
                if 0 <= b < NB:
                    r = slice(b % 2, b % 2 + 1)
                    dve.wait_ge(xs_exp, b + 1)
                    dve.reciprocal(xinv[:, r], xsum[:, r]).then_inc(xs_inv, 1)
                    dve.wait_ge(xs_inv, b + 1)
                    dve.tensor_scalar(xprobs[:, b % 2, :], xprobs[:, b % 2, :], xinv[:, r], None,
                                      ALU.mult).then_inc(xs_prob, 1)

            def cross_last(t):
                b = t - AT_CONTEXT
                if 0 <= b < NB:
                    dve.wait_ge(xc_done, b + 1)
                    dve.tensor_tensor(xacc[:, b, :], psum[:, BK_XC, :], xacc[:, b, :],
                                      ALU.add).then_inc(x_added, 1)
                    dve.wait_ge(x_added, b + 1)
                    count(b, 2)

            def group(g, more):
                step = g * NB
                for t in range(SLOTS + 1):
                    if t < NB:
                        r = t % 2
                        dve.wait_ge(score_done, step + t + 1 + PRIME)
                        dve.wait_ge(pt_done, step + t - 1 + PRIME)
                        dve.tensor_tensor(probs[:, r], psum[:, BK_S, :].rearrange("p (a b) -> p a b", a=HG),
                                          causal[:].unsqueeze(1).to_broadcast([P, HG, P]),
                                          ALU.add).then_inc(masked, 1)
                        dve.wait_ge(masked, step + t + 1 + PRIME)
                        dve.tensor_reduce(rowmax[:, r, :], probs[:, r], AX_X, ALU.max).then_inc(maxed, 1)
                        dve.wait_ge(maxed, step + t + 1)
                        dve.tensor_scalar(negmax[:, r, :], rowmax[:, r, :], -SCALE, None,
                                          ALU.mult).then_inc(neg_ready, 1)
                    if 1 <= t <= NB:
                        u = t - 1
                        dve.wait_ge(pthi_ready, step + u + 1)
                        dve.tensor_tensor(pt_lo[:], psum[:, BK_T, :].rearrange("p (a b) -> p a b", a=HG),
                                          pt_hi[:].bitcast(F32), ALU.subtract).then_inc(ptlo_ready, 1)
                    if not more:
                        cross_max(t)
                    if t >= 3:
                        u = t - 3
                        dve.wait_ge(o_done, step + u + 1 + PRIME)
                        dve.tensor_tensor(xacc[:, u, :], psum[:, BK_O, :], xacc[:, u, :],
                                          ALU.add).then_inc(o_added, 1)
                    if t < NB:
                        dve.wait_ge(exp_done, step + t + 1)
                        dve.reciprocal(rowinv[:, t % 2, :], rowsum[:, t % 2, :]).then_inc(inv_ready, 1)
                    if not more:
                        cross_inverse(t)
                    if t in TURN_V and (more or TURN_V[t] == 1):
                        dve.wait_ge(vt_hi, g * NH + (3 - TURN_V[t]))
                        v_second(TURN_V[t])
                    if 1 <= t <= NB:
                        u = t - 1
                        dve.wait_ge(athi_ready, step + u + 1)
                        dve.tensor_tensor(at_lo[:, u % 2], psum[:, BK_PV, :].rearrange("p (a b) -> p a b", a=HG),
                                          at_hi[:, u % 2].bitcast(F32), ALU.subtract).then_inc(atlo_ready, 1)
                    if not more:
                        if t >= 3:
                            dve.wait_ge(o_added, step + t - 2 + PRIME)
                            count(t - 3, 1)
                        cross_last(t)
                        if t in (1, 2):
                            unpack(t - 1, 0, P, TILE_LOADS, t - 1, 3 * (t - 1), t > 1)

            dve.wait_ge(consts_dve, 1)
            TILE_LOADS = 16 * 2 * (HC + 2)
            DOWN_LOADS = 16 * 3

            def unpack(m, r, w, loads, unit, group_step, free, down=False):
                dve.wait_ge(ld_f[r], loads)
                if down:
                    q, z = f_q[0:w, r, 0], f_z[0:w, r, 0].rearrange("p a b -> p (a b)")
                    zn, dst = f_zn[0:w].rearrange("p a b -> p (a b)"), f_m[0:w, m]
                    zb = z.unsqueeze(2).to_broadcast([w, H // NIBBLES, NIBBLES])
                    zo = zn.rearrange("p (a b) -> p a b", b=NIBBLES)
                    sh = z_shift[0:w].unsqueeze(1).to_broadcast([w, H // NIBBLES, NIBBLES])
                    zn = f_zn[0:w]
                    rows = w
                else:
                    zw = w // NIBBLES
                    q, z = f_q[:, r, m, :, 0:w], f_z[:, r, m, :, 0:zw]
                    zn, dst = f_zn[:, :, 0:w], f_m[:, m, :, 0:w]
                    zb = z.unsqueeze(3).to_broadcast([P, HC, zw, NIBBLES])
                    zo = zn.rearrange("p c (a b) -> p c a b", b=NIBBLES)
                    sh = z_shift[:].unsqueeze(1).unsqueeze(1).to_broadcast([P, HC, zw, NIBBLES])
                    rows = P
                if free:
                    dve.wait_ge(fm_ready, unit)
                dve.tensor_scalar(q, q, q_shift[0:rows, 0:1], 15, ALU.logical_shift_right,
                                  ALU.bitwise_and).then_inc(fq_step, 1)
                dve.tensor_tensor(zo, zb, sh, ALU.logical_shift_right).then_inc(fq_step, 1)
                dve.wait_ge(fq_step, group_step + 2)
                dve.tensor_scalar(zn, zn, 15, None, ALU.bitwise_and).then_inc(fq_step, 1)
                dve.wait_ge(fq_step, group_step + 3)
                if not isinstance(unit, int) or unit >= 2:
                    dve.wait_ge(fw_ready, unit - 1)
                dve.scalar_tensor_tensor(dst, q, -1.0, zn, ALU.add, ALU.subtract).then_inc(fm_ready, 1)

            with dve.Fori(0, LAST) as g:
                group(g, True)
            group(LAST, False)

            for t in range(SLOTS + 1, ALL_SLOTS + 1):
                cross_max(t)
                cross_inverse(t)
                cross_last(t)
            for m in range(2):
                unpack(m, 1, P, TILE_LOADS, 2 + m, 6 + 3 * m, True)

            def tile_weights(n, r, w, uses):
                for m in range(2):
                    unpack(m, r, w, uses * TILE_LOADS + TILE_LOADS, n * 2 + m, n * 6 + 3 * m, True)

            def down_weights(c):
                r = (NT + c) % 2
                tiles = (NT + 1 - r) // 2
                loads = tiles * TILE_LOADS + (c // 2 + 1) * DOWN_LOADS
                unpack(c % 2, r, width(c), loads, 2 * NT + c, 6 * NT + 3 * c, True, down=True)

            def inner(n, r, w):
                gate = psum[0:w, 4 * r:4 * r + 2, :].rearrange("p a b -> p (a b)")
                up = psum[0:w, 4 * r + 2:4 * r + 4, :].rearrange("p a b -> p (a b)")
                dve.wait_ge(sig_ready, n + 1)
                dve.tensor_tensor(f_sig[0:w, :], gate, f_sig[0:w, :], ALU.mult).then_inc(gs_ready, 1)
                dve.wait_ge(gs_ready, n + 1)
                dve.wait_ge(gu_done, n * 2 + 2 + PRIME)
                dve.wait_ge(intlo_ready, n + PRIME)
                dve.tensor_tensor(f_int[0:w, :], up, f_sig[0:w, :], ALU.mult).then_inc(int_ready, 1)

            with dve.Fori(0, (NT - 3) // 2) as pair:
                for r in range(2):
                    n = pair * 2 + r
                    tile_weights(n + 2, r, P, pair + 1)
                    inner(n, r, P)
            for n in range(NT - 3, NT):
                if n + 2 < NT:
                    tile_weights(n + 2, n % 2, width(n + 2), (n + 2) // 2)
                else:
                    down_weights(n + 2 - NT)
                inner(n, n % 2, width(n))
            for c in range(2, NT):
                down_weights(c)
            for b in range(NB):
                dve.wait_ge(y16_ready, b + 1)
                dve.tensor_tensor(xacc[:, b, :], xacc[:, b, :], y16[:, b % 2, :], ALU.add).then_inc(y_ready, 1)


_INS = ["x", "ctx_4096", "L0_attn_w_q", "L0_attn_w_k", "L0_attn_w_v", "L0_attn_w_o",
        "L0_ffn_gate_qweight", "L0_ffn_gate_scales", "L0_ffn_gate_zeros",
        "L0_ffn_up_qweight", "L0_ffn_up_scales", "L0_ffn_up_zeros",
        "L0_ffn_down_qweight", "L0_ffn_down_scales", "L0_ffn_down_zeros"]


def kernel(**inputs):
    import numpy as np
    import concourse.bacc as bacc
    from concourse.bass_utils import run_bass_kernel_spmd

    nc = bacc.Bacc("TRN2", target_bir_lowering=False, num_devices=1)
    arrays, args = {}, []
    for name in _INS:
        a = np.ascontiguousarray(inputs[name])
        arrays[f"in_{name}"] = a
        args.append(nc.dram_tensor(f"in_{name}", a.shape, mybir.dt.from_np(a.dtype), kind="ExternalInput").ap())
    shape = inputs["x"].shape
    args.append(nc.dram_tensor("out_0", shape, F32, kind="ExternalOutput").ap())
    decoder_kernel(nc, *args)
    got = run_bass_kernel_spmd(nc, [arrays], core_ids=[0])
    return got.results[0]["out_0"]
```

```python
from contextlib import ExitStack

import concourse.bass as bass
from concourse import mybir

ALU = mybir.AluOpType
ACT = mybir.ActivationFunctionType
AX_X = mybir.AxisListType.X
F32 = mybir.dt.float32
F32R = mybir.dt.float32r
F16 = mybir.dt.float16
I32 = mybir.dt.int32

P = 128
EPS = 1e-5
MASKED = -1e30
NIBBLES = 8
PRIME = 2


def decoder_kernel(nc, x, ctx_in, w_q, w_k, w_v, w_o,
                   gate_q, gate_s, gate_z, up_q, up_s, up_z, down_q, down_s, down_z, out):
    NB, S, H = x.shape
    T = NB * S
    HC = H // P
    NG = w_k.shape[1] // P
    HG = w_q.shape[1] // w_k.shape[1]
    HALF = 512
    NH = T // HALF
    BH = HALF // S
    INTER = gate_q.shape[1]
    NT = (INTER + P - 1) // P
    SCALE = float(P) ** -0.5
    assert S == P and H == HALF and NH == 2 and HG == 4 and NG % 2 == 0

    HBLK = ["k", "v"] + [f"q{j}" for j in range(HG)]
    BLOCKS = [(u, 1) for u in HBLK] + [(u, 0) for u in HBLK]
    NBLK = len(BLOCKS)
    FILL = {0: [0, 1], 1: [2, 3], 2: [4], 3: [5], 4: [6], 5: [7], 6: [8], 7: [9], 8: [10], 9: [11]}
    TURN_V = {1: 1, 6: 0}
    CTX_FILL = {t: (2 * (t - 2), 2 * (t - 2) + 1) for t in range(2, 2 + NB // 2)}
    SLOTS = NB + 2
    AT_NORM2, AT_SIM, AT_NORM3 = 3, 4, 6
    ALL_SLOTS = NB + AT_NORM3
    EARLY = 4
    EARLY_TILES = 2
    EARLY_UNPACK = {0: 0, 1: 1, 8: 2, 9: 3}
    EARLY_SCALE = {1: 0, 2: 1, 8: 2, 9: 3}
    EARLY_SECOND = {4: 0, 5: 1, 9: 2, 10: 3}
    SPLIT = {0: ["o0", "o1"], 1: ["o2", "o3"], 2: ["k"], 3: ["v"], 4: ["q0"], 5: ["q1"], 6: ["q2"], 7: ["q3"]}
    FIRST_UNITS = len(HBLK)
    UNITS = len(HBLK) + HG

    with ExitStack() as stack:
        def sem(name):
            return stack.enter_context(nc.semaphore(name))

        def allocator(scope):
            return lambda name, shape, dt=F32: scope.enter_context(nc.sbuf_tensor(name, shape, dt))

        sb = allocator(stack)
        xacc = sb("xacc", [P, NB, H])
        xn = sb("xn", [P, 2, H])
        ident = sb("ident", [P, P])
        causal = sb("causal", [P, P])
        stats = sb("stats", [P, NB, 6])
        meanvar = sb("meanvar", [P, NB, 2])
        vareps = sb("vareps", [P, NB])
        shift = sb("shift", [P, NB])
        halfneg = sb("halfneg", [P, 1])
        xm = sb("xm", [P, 2, H])
        f_q = sb("f_q", [P, 2, 2, HC, P], I32)
        f_z = sb("f_z", [P, 2, 2, HC, P // NIBBLES], I32)
        f_s = sb("f_s", [P, 2, 2, HC, P], F16)
        f_zn = sb("f_zn", [P, HC, P], I32)
        f_m = sb("f_m", [P, 2, HC, P])
        f_w = sb("f_w", [P, 2, HC, P])
        rstd = sb("rstd", [P, NB])
        newton = sb("newton", [P, NB])
        rowmax = sb("rowmax", [P, 2, HG])
        negmax = sb("negmax", [P, 2, HG])
        rowsum = sb("rowsum", [P, 2, HG])
        rowinv = sb("rowinv", [P, 2, HG])
        xmax = sb("xmax", [P, 2])
        xneg = sb("xneg", [P, 2])
        xsum = sb("xsum", [P, 2])
        xinv = sb("xinv", [P, 2])
        part_i = sb("part_i", [P, 1], I32)
        q_shift = sb("q_shift", [P, 1], I32)
        z_shift = sb("z_shift", [P, NIBBLES], I32)
        psum = stack.enter_context(nc.psum_tensor("psum", [P, 8, HALF], F32))
        BK_S, BK_T, BK_PV, BK_O, BK_VT, BK_PROJ = 0, 2, 4, 6, 1, (3, 5)
        BK_XT, BK_XS, BK_XC, BK_FT = BK_VT, 7, 3, 5
        CTX_BANK = [BK_XS] * 4 + [BK_FT] * 4

        def gate_up_bank(r, m, h):
            return 4 * r + 2 * m + h


        with ExitStack() as scope:
            sb = allocator(scope)
            xt_hi = sb("xt_hi", [P, HC, T], F32R)
            xt_lo = sb("xt_lo", [P, HC, T], F32R)
            wq_hi = sb("wq_hi", [P, HG, HC, P], F32R)
            wq_lo = sb("wq_lo", [P, HG, HC, P], F32R)
            wk_hi = sb("wk_hi", [P, HC, P], F32R)
            wk_lo = sb("wk_lo", [P, HC, P], F32R)
            wv_hi = sb("wv_hi", [P, HC, P], F32R)
            wv_lo = sb("wv_lo", [P, HC, P], F32R)
            wq_raw = sb("wq_raw", [P, HC, HG * P])
            wk_raw = sb("wk_raw", [P, HC, P])
            wv_raw = sb("wv_raw", [P, HC, P])
            wo_raw = sb("wo_raw", [P, HG, H])
            wo_hi = sb("wo_hi", [P, HG, H], F32R)
            wo_lo = sb("wo_lo", [P, HG, H], F32R)
            qt = sb("qt", [P, HG, T])
            kt = sb("kt", [P, T])
            vt = sb("vt", [P, HALF])
            v_hi = sb("v_hi", [P, NB, P], F32R)
            v_lo = sb("v_lo", [P, NB, P], F32R)
            probs = sb("probs", [P, 2, HG, P])
            pt_hi = sb("pt_hi", [P, HG, P], F32R)
            pt_lo = sb("pt_lo", [P, HG, P], F32R)
            at_hi = sb("at_hi", [P, 2, HG, P], F32R)
            at_lo = sb("at_lo", [P, 2, HG, P], F32R)
            cx = sb("cx", [P, NB, H])
        with ExitStack() as scope:
            sb = allocator(scope)
            ft_hi = sb("ft_hi", [P, HC, T], F32R)
            ft_lo = sb("ft_lo", [P, HC, T], F32R)
            f_hi = sb("f_hi", [P, 2, 2, HC, P], F32R)
            f_lo = sb("f_lo", [P, 2, 2, HC, P], F32R)
            with ExitStack() as cross_scope:
                sb = allocator(cross_scope)
                cxt = sb("cxt", [P, HC, T])
                query_t = sb("query_t", [P, 2, HC, P])
                xprobs = sb("xprobs", [P, 2, P])
            sb = allocator(scope)
            f_sig = sb("f_sig", [P, T])
            f_int = sb("f_int", [P, T])
            y16 = sb("y16", [P, 2, H], F16)
            int_hi = sb("int_hi", [P, NT, T], F32R)
            int_lo = sb("int_lo", [P, NT, T], F32R)

        ld_x = [sem(f"ld_x{b}") for b in range(NB)]
        ld_w = {k: sem(f"ld_w{k}") for k in "qkvo"}
        ld_cx = sem("ld_cx")
        consts_pool = sem("consts_pool")
        consts_dve = sem("consts_dve")
        stat_step = sem("stat_step")
        var_ready = [sem(f"var_ready{i}") for i in range(3)]
        rstd_step = sem("rstd_step")
        rstd_ready = [sem(f"rstd_ready{i}") for i in range(3)]
        ln_ready = [sem(f"ln_ready{i}") for i in range(3)]
        ln_turned = [sem(f"ln_turned{i}") for i in range(3)]
        ln_hi = [sem(f"ln_hi{i}") for i in range(3)]
        ln_lo = [sem(f"ln_lo{i}") for i in range(3)]
        w_hi = sem("w_hi")
        w_lo = sem("w_lo")
        proj_done = sem("proj_done")
        proj_out = sem("proj_out")
        vt_done = sem("vt_done")
        vt_hi = sem("vt_hi")
        vt_lo = sem("vt_lo")
        score_done = sem("score_done")
        masked = sem("masked")
        maxed = sem("maxed")
        neg_ready = sem("neg_ready")
        exp_done = sem("exp_done")
        inv_ready = sem("inv_ready")
        prob_ready = sem("prob_ready")
        pt_done = sem("pt_done")
        pthi_ready = sem("pthi_ready")
        ptlo_ready = sem("ptlo_ready")
        pv_done = sem("pv_done")
        athi_ready = sem("athi_ready")
        atlo_ready = sem("atlo_ready")
        o_done = sem("o_done")
        o_added = sem("o_added")
        cx_turned = sem("cx_turned")
        cx_out = sem("cx_out")
        xs_done = sem("xs_done")
        xs_max = sem("xs_max")
        xs_neg = sem("xs_neg")
        xs_exp = sem("xs_exp")
        xs_inv = sem("xs_inv")
        xs_prob = sem("xs_prob")
        xc_done = sem("xc_done")
        x_added = sem("x_added")
        ld_f = [sem(f"ld_f{i}") for i in range(2)]
        fq_step = sem("fq_step")
        fm_ready = sem("fm_ready")
        fw_ready = sem("fw_ready")
        fhi_ready = sem("fhi_ready")
        flo_ready = sem("flo_ready")
        gu_done = sem("gu_done")
        sig_ready = sem("sig_ready")
        gs_ready = sem("gs_ready")
        int_ready = sem("int_ready")
        inthi_ready = sem("inthi_ready")
        intlo_ready = sem("intlo_ready")
        down_done = sem("down_done")
        y16_ready = sem("y16_ready")
        y_ready = sem("y_ready")
        stored = sem("stored")

        FIRST_BLOCKS = len(HBLK)
        CTX_BLOCKS = NG * NBLK
        LAST = NG - 1
        ATT = NG * NB
        TILES = NB

        def weight(unit, raw=False):
            kind, j = unit[0], int(unit[1:] or 0)
            if raw:
                return {"k": lambda: wk_raw[:], "v": lambda: wv_raw[:],
                        "q": lambda: wq_raw[:, :, j * P:(j + 1) * P], "o": lambda: wo_raw[:, j]}[kind]()
            return {"k": lambda: (wk_hi[:], wk_lo[:]), "v": lambda: (wv_hi[:], wv_lo[:]),
                    "q": lambda: (wq_hi[:, j], wq_lo[:, j]), "o": lambda: (wo_hi[:, j], wo_lo[:, j])}[kind]()

        def width(n):
            return min(P, INTER - n * P)

        block = stack.enter_context(nc.Block())

        @block.sync
        def _(sp):
            wq_v = w_q.rearrange("(c p) n -> p c n", p=P)
            wk_v = w_k.rearrange("(c p) n -> p c n", p=P)
            wv_v = w_v.rearrange("(c p) n -> p c n", p=P)
            wo_v = w_o.rearrange("(h p) n -> p h n", p=P)

            def load_w(kind, g):
                dst, src = {
                    "q": (wq_raw, lambda: wq_v[:, :, g * HG * P:(g + 1) * HG * P]),
                    "k": (wk_raw, lambda: wk_v[:, :, g * P:(g + 1) * P]),
                    "v": (wv_raw, lambda: wv_v[:, :, g * P:(g + 1) * P]),
                    "o": (wo_raw, lambda: wo_v[:, g * HG:(g + 1) * HG, :]),
                }[kind]
                sp.dma_start(dst[:], src()).then_inc(ld_w[kind], 16)

            def load_ffn(n):
                r, c0, w = n % 2, n * P, width(n)
                for m, (q, s, z) in enumerate(((gate_q, gate_s, gate_z), (up_q, up_s, up_z))):
                    for c in range(HC):
                        rows = q[c * P // NIBBLES:(c + 1) * P // NIBBLES, c0:c0 + w]
                        sp.dma_start(f_q[:, r, m, c, 0:w],
                                     rows.unsqueeze(1).to_broadcast([P // NIBBLES, NIBBLES, w])
                                     ).then_inc(ld_f[r], 16)
                    sp.dma_start(f_s[:, r, m, :, 0:w],
                                 s[:, c0:c0 + w].unsqueeze(0).to_broadcast([P, HC, w])).then_inc(ld_f[r], 16)
                    zc, zw = c0 // NIBBLES, w // NIBBLES
                    sp.dma_start(f_z[:, r, m, :, 0:zw],
                                 z[:, zc:zc + zw].unsqueeze(0).to_broadcast([P, HC, zw])).then_inc(ld_f[r], 16)

            def load_down(c):
                r, w = (NT + c) % 2, width(c)
                rows = down_q[c * P // NIBBLES:(c * P + w) // NIBBLES, :]
                sp.dma_start(f_q[0:w, r, 0].rearrange("p a b -> p (a b)"),
                             rows.unsqueeze(1).to_broadcast([w // NIBBLES, NIBBLES, H])).then_inc(ld_f[r], 16)
                sp.dma_start(f_s[0:w, r, 0].rearrange("p a b -> p (a b)"),
                             down_s[c:c + 1, :].to_broadcast([w, H])).then_inc(ld_f[r], 16)
                sp.dma_start(f_z[0:w, r, 0].rearrange("p a b -> p (a b)"),
                             down_z[c:c + 1, :].to_broadcast([w, H // NIBBLES])).then_inc(ld_f[r], 16)

            for b in range(NB):
                sp.dma_start(xacc[:, b, :], x[b]).then_inc(ld_x[b], 16)
                if b == BH - 1:
                    load_w("k", 0)
                    load_w("v", 0)
                    load_w("q", 0)
            load_w("o", 0)
            load_ffn(0)
            load_ffn(1)
            sp.dma_start(cx[:], ctx_in.rearrange("b c s -> c b s")).then_inc(ld_cx, 16)
            for g in range(NG):
                before = g * UNITS + (0 if g == 0 else HG)
                if g + 1 < NG:
                    sp.wait_ge(w_lo, before + 1)
                    load_w("k", g + 1)
                    sp.wait_ge(w_lo, before + 2)
                    load_w("v", g + 1)
                    sp.wait_ge(w_lo, before + 2 + HG)
                    load_w("q", g + 1)
                    sp.wait_ge(w_lo, g * UNITS + FIRST_UNITS + HG)
                    load_w("o", g + 1)

            for n in range(2, NT):
                sp.wait_ge(fm_ready, 2 * (n - 1))
                sp.wait_ge(fw_ready, 2 * (n - 1))
                load_ffn(n)
            for c in range(NT):
                done = 2 * (NT - 1) if c == 0 else 2 * NT + c - 1
                sp.wait_ge(fm_ready, done)
                sp.wait_ge(fw_ready, done)
                load_down(c)
            for b in range(NB):
                sp.wait_ge(y_ready, b + 1)
                sp.dma_start(out[b], xacc[:, b, :]).then_inc(stored, 16)
            sp.wait_ge(stored, 16 * NB)

        @block.tensor
        def _(pe):
            for s in (score_done, pt_done, pv_done, o_done, gu_done):
                pe.sem_inc(s, PRIME)

            def passes(dst, a_hi, a_lo, b_hi, b_lo, start, stop):
                pe.matmul(dst, a_hi, b_hi, start=start, stop=False)
                pe.matmul(dst, a_hi, b_lo, start=False, stop=False)
                return pe.matmul(dst, a_lo, b_hi, start=False, stop=stop)

            def turn_tile(bank, src):
                for c in range(HC):
                    mm = pe.transpose(psum[:, bank, c * P:(c + 1) * P], src[:, c * P:(c + 1) * P], ident[:])
                return mm

            def project(unit, n, bank):
                hi, lo = weight(unit)
                cols = slice(n * HALF, (n + 1) * HALF)
                for c in range(HC):
                    mm = passes(psum[:, bank, :], hi[:, c, :], lo[:, c, :], xt_hi[:, c, cols],
                                xt_lo[:, c, cols], c == 0, c == HC - 1)
                mm.then_inc(proj_done, 1)

            def turn_v():
                for k in range(BH):
                    mm = pe.transpose(psum[:, BK_VT, k * P:(k + 1) * P], vt[:, k * P:(k + 1) * P], ident[:])
                mm.then_inc(vt_done, 1)

            pe.wait_ge(consts_pool, 4)
            for b in range(NB):
                pe.wait_ge(ln_ready[0], b + 1)
                if b >= 2:
                    pe.wait_ge(ln_lo[0], b - 1)
                turn_tile((BK_T, BK_VT)[b % 2], xn[:, b % 2, :]).then_inc(ln_turned[0], 1)
                if b >= BH:
                    i = b - BH
                    pe.wait_ge(ln_lo[0], max(BH, b - 1))
                    pe.wait_ge(w_lo, i + 1)
                    if i >= 2:
                        pe.wait_ge(proj_out, i - 1)
                    project(HBLK[i], 0, BK_PROJ[i % 2])
            pe.wait_ge(ln_lo[0], NB)
            pe.wait_ge(proj_out, 2)
            turn_v()
            for i in range(NB - BH, FIRST_BLOCKS):
                pe.wait_ge(w_lo, i + 1)
                pe.wait_ge(proj_out, i - 1)
                project(HBLK[i], 0, BK_PROJ[i % 2])

            def out_heads(g, u):
                step = g * NB
                pe.wait_ge(atlo_ready, step + u + 1 + PRIME)
                pe.wait_ge(w_lo, g * UNITS + FIRST_UNITS + HG)
                pe.wait_ge(o_added, step + u + PRIME)
                for j in range(HG):
                    mm = passes(psum[:, BK_O, :], at_hi[:, u % 2, j, :], at_lo[:, u % 2, j, :],
                                wo_hi[:, j, :], wo_lo[:, j, :], j == 0, j == HG - 1)
                mm.then_inc(o_done, 1)

            def turn_context(t, k):
                if t in CTX_FILL:
                    b = CTX_FILL[t][k]
                    if b == 0:
                        pe.wait_ge(ld_cx, 16)
                    elif CTX_BANK[b] == CTX_BANK[b - 1]:
                        pe.wait_ge(cx_out, b)
                    else:
                        pe.wait_ge(proj_out, CTX_BLOCKS)
                    turn_tile(CTX_BANK[b], cx[:, b, :]).then_inc(cx_turned, 1)

            def cross_scores(t):
                b = t - AT_SIM
                if 0 <= b < NB:
                    pe.wait_ge(ln_hi[1], b + 1)
                    pe.wait_ge(cx_out, max(b + 1, CTX_BANK.index(BK_FT)))
                    if b >= 1:
                        pe.wait_ge(xs_exp, b)
                    for c in range(HC):
                        mm = pe.matmul(psum[:, BK_XS, 0:P], query_t[:, b % 2, c, :],
                                       cxt[:, c, b * P:(b + 1) * P], start=(c == 0), stop=(c == HC - 1))
                    mm.then_inc(xs_done, 1)

            def turn_queries(t):
                b = t - AT_NORM2
                if 0 <= b < NB:
                    pe.wait_ge(ln_ready[1], b + 1)
                    if b >= 1:
                        pe.wait_ge(ln_hi[1], b)
                    else:
                        pe.wait_ge(vt_lo, NG * NH)
                    turn_tile(BK_XT, xn[:, b % 2, :]).then_inc(ln_turned[1], 1)

            def cross_output(t):
                b = t - AT_SIM
                if 0 <= b < NB:
                    pe.wait_ge(xs_prob, b + 1)
                    if b == 0:
                        pe.wait_ge(proj_out, CTX_BLOCKS)
                    else:
                        pe.wait_ge(x_added, b)
                    pe.matmul(psum[:, BK_XC, :], xprobs[:, b % 2, :], cx[:, b, :],
                              start=True, stop=True).then_inc(xc_done, 1)

            def turn_third(t):
                b = t - AT_NORM3
                if 0 <= b < NB:
                    pe.wait_ge(ln_ready[2], b + 1)
                    if b >= 1:
                        pe.wait_ge(ln_lo[2], b)
                    else:
                        pe.wait_ge(cx_out, NB)
                    turn_tile(BK_FT, xm[:, b % 2, :]).then_inc(ln_turned[2], 1)

            def group(g, more):
                step, blocks = g * NB, g * NBLK + FIRST_BLOCKS
                for t in range(SLOTS):
                    if t < NB:
                        pe.wait_ge(masked, step + t + PRIME)
                        pe.wait_ge(proj_out, blocks + (0 if t < BH else len(HBLK)))
                        for j in range(HG):
                            mm = pe.matmul(psum[:, BK_S, j * P:(j + 1) * P],
                                           qt[:, j, t * P:(t + 1) * P], kt[:, t * P:(t + 1) * P],
                                           start=True, stop=True)
                        mm.then_inc(score_done, 1)
                    if 1 <= t <= NB:
                        u = t - 1
                        pe.wait_ge(prob_ready, step + u + 1)
                        pe.wait_ge(ptlo_ready, step + u + PRIME)
                        for j in range(HG):
                            mm = pe.transpose(psum[:, BK_T, j * P:(j + 1) * P], probs[:, u % 2, j, :], ident[:])
                        mm.then_inc(pt_done, 1)
                    if t in TURN_V and (more or TURN_V[t] == 1):
                        n = TURN_V[t]
                        i = BLOCKS.index(("v", n))
                        pe.wait_ge(proj_out, blocks + i + 1)
                        pe.wait_ge(vt_lo, g * NH + (2 - n))
                        turn_v()
                    if not more:
                        turn_context(t, 0)
                    for i in FILL[t]:
                        unit, n = BLOCKS[i]
                        if n == 0 and not more:
                            continue
                        k = HBLK.index(unit)
                        pe.wait_ge(w_lo, g * UNITS + (k + 1 if n == 1 else FIRST_UNITS + HG + k + 1))
                        pe.wait_ge(proj_out, blocks + i - 1)
                        project(unit, n, BK_PROJ[i % 2])
                    if not more:
                        cross_scores(t)
                        if t >= EARLY:
                            out_heads(g, t - 2)
                    if 1 <= t <= NB:
                        u = t - 1
                        pe.wait_ge(ptlo_ready, step + u + 1 + PRIME)
                        pe.wait_ge(vt_lo, g * NH + (1 if u < BH else 2))
                        pe.wait_ge(atlo_ready, step + u + PRIME)
                        passes(psum[:, BK_PV, :], v_hi[:, u, :], v_lo[:, u, :],
                               pt_hi[:].rearrange("p a b -> p (a b)"), pt_lo[:].rearrange("p a b -> p (a b)"),
                               True, True).then_inc(pv_done, 1)
                    if t >= 2 and (more or t < EARLY):
                        out_heads(g, t - 2)
                    if not more:
                        turn_third(t)
                        turn_queries(t)
                        turn_context(t, 1)
                        cross_output(t)

            with pe.Fori(0, LAST) as g:
                group(g, True)
            group(LAST, False)

            def gate_up(n, r, w, m, h):
                pe.wait_ge(flo_ready, n * 2 + m + 1)
                for c in range(HC):
                    cols = slice(h * HALF, (h + 1) * HALF)
                    mm = passes(psum[0:w, gate_up_bank(r, m, h), :], f_hi[:, r, m, c, 0:w],
                                f_lo[:, r, m, c, 0:w], ft_hi[:, c, cols], ft_lo[:, c, cols],
                                c == 0, c == HC - 1)
                if h == NH - 1:
                    mm.then_inc(gu_done, 1)

            def inner_tile(n, r, w):
                pe.wait_ge(int_ready, n + PRIME - 1)
                for m in range(2):
                    for h in range(NH):
                        gate_up(n, r, w, m, h)

            for t in range(SLOTS, ALL_SLOTS):
                cross_scores(t)
                k = t - SLOTS
                if k == 0:
                    pe.wait_ge(ln_lo[2], BH)
                    pe.wait_ge(o_added, ATT + PRIME)
                if k < EARLY_TILES * 2:
                    gate_up(k // 2, k // 2, P, k % 2, 0)
                turn_queries(t)
                cross_output(t)
                turn_third(t)
            pe.wait_ge(ln_lo[2], NB)
            for n in range(EARLY_TILES):
                for m in range(2):
                    gate_up(n, n, P, m, 1)
            with pe.Fori(0, (NT - 3 - EARLY_TILES) // 2) as pair:
                for r in range(2):
                    inner_tile(pair * 2 + EARLY_TILES + r, r, P)
            for n in range(NT - 3, NT):
                inner_tile(n, n % 2, width(n))

            last_r = (NT - 1) % 2
            free_last = [gate_up_bank(last_r, m, h) for h in range(NH) for m in range(2)]
            free_first = [b for b in range(NB) if b not in free_last]
            for c in range(NT):
                w, r, m = width(c), (NT + c) % 2, (c // 2) % 2
                pe.wait_ge(flo_ready, 2 * NT + c + 1)
                pe.wait_ge(intlo_ready, c + 1 + PRIME)
                for b in free_first + free_last if c == 0 else range(NB):
                    if c == 0 and b == free_first[0]:
                        pe.wait_ge(int_ready, NT - 1 + PRIME)
                    if c == 0 and b == free_last[0]:
                        pe.wait_ge(int_ready, NT + PRIME)
                    mm = passes(psum[:, b, :], int_hi[0:w, c, b * P:(b + 1) * P], int_lo[0:w, c, b * P:(b + 1) * P],
                                f_hi[0:w, r, m].rearrange("p a b -> p (a b)"),
                                f_lo[0:w, r, m].rearrange("p a b -> p (a b)"), c == 0, c == NT - 1)
                    if c == NT - 1:
                        mm.then_inc(down_done, 1)
                if c < NT - 1:
                    mm.then_inc(gu_done, 1)

        @block.scalar
        def _(act):
            def split_first(unit):
                act.copy(weight(unit)[0], weight(unit, raw=True)).then_inc(w_hi, 1)

            def tile_first(b, k, hi, bank):
                act.wait_ge(ln_turned[k], b + 1)
                act.copy(hi[:, :, b * P:(b + 1) * P],
                         psum[:, bank, :].rearrange("p (c t) -> p c t", c=HC)).then_inc(ln_hi[k], 1)

            def project_out(unit, n, bank):
                cols = slice(n * HALF, (n + 1) * HALF)
                dst = vt[:] if unit == "v" else kt[:, cols] if unit == "k" else qt[:, int(unit[1:]), cols]
                act.copy(dst, psum[:, bank, :]).then_inc(proj_out, 1)

            def v_first(n):
                act.copy(v_hi[:, n * BH:(n + 1) * BH, :],
                         psum[:, BK_VT, :].rearrange("p (a b) -> p a b", a=BH)).then_inc(vt_hi, 1)

            def first_unit(i):
                act.wait_ge(ld_w[HBLK[i][0]], 16)
                split_first(HBLK[i])

            def normalise(b, k, dst):
                act.wait_ge(rstd_ready[k], b + 1)
                if b >= 2:
                    act.wait_ge(ln_turned[k], b - 1)
                act.activation(dst[:, b % 2, :], xacc[:, b, :], ACT.Identity, bias=shift[:, b:b + 1],
                               scale=rstd[:, b:b + 1]).then_inc(ln_ready[k], 1)

            for i in range(NB + 1):
                if i < NB:
                    normalise(i, 0, xn)
                if i >= 1:
                    tile_first(i - 1, 0, xt_hi, (BK_T, BK_VT)[(i - 1) % 2])
                if 1 <= i <= FIRST_UNITS:
                    first_unit(i - 1)
                if i >= BH + 2:
                    j = i - BH - 2
                    act.wait_ge(proj_done, j + 1)
                    project_out(HBLK[j], 0, BK_PROJ[j % 2])
            for i in range(NB - BH - 1, FIRST_BLOCKS):
                if i == 3:
                    act.wait_ge(vt_done, 1)
                    v_first(0)
                act.wait_ge(proj_done, i + 1)
                project_out(HBLK[i], 0, BK_PROJ[i % 2])

            def context_first(t, k):
                if t in CTX_FILL:
                    b = CTX_FILL[t][k]
                    act.wait_ge(cx_turned, b + 1)
                    act.copy(cxt[:, :, b * P:(b + 1) * P],
                             psum[:, CTX_BANK[b], :].rearrange("p (c t) -> p c t", c=HC)).then_inc(cx_out, 1)

            def cross_exp(t):
                b = t - AT_SIM
                if 0 <= b < NB:
                    act.wait_ge(xs_neg, b + 1)
                    if b >= 2:
                        act.wait_ge(xc_done, b - 1)
                    act.activation(xprobs[:, b % 2, :], psum[:, BK_XS, 0:P], ACT.Exp,
                                   bias=xneg[:, b % 2:b % 2 + 1], scale=SCALE,
                                   accum_out=xsum[:, b % 2:b % 2 + 1]).then_inc(xs_exp, 1)
                b = t - AT_NORM2
                if 0 <= b < NB:
                    normalise(b, 1, xn)

            def third_norm(t):
                b = t - AT_NORM3
                if 0 <= b < NB:
                    normalise(b, 2, xm)

            def queries_out(t):
                b = t - AT_NORM2
                if 0 <= b < NB:
                    act.wait_ge(ln_turned[1], b + 1)
                    if b >= 2:
                        act.wait_ge(xs_done, b - 1)
                    act.copy(query_t[:, b % 2], psum[:, BK_XT, :].rearrange("p (c t) -> p c t", c=HC)
                             ).then_inc(ln_hi[1], 1)

            def third(t):
                b = t - AT_NORM3
                if 0 <= b < NB:
                    tile_first(b, 2, ft_hi, BK_FT)

            def early_first(unit):
                act.wait_ge(fw_ready, unit + 1)
                act.wait_ge(proj_done, CTX_BLOCKS)
                act.copy(f_hi[:, unit // 2, unit % 2], f_w[:, unit % 2]).then_inc(fhi_ready, 1)

            def group(g, more):
                step, blocks = g * NB, g * NBLK + FIRST_BLOCKS
                for t in range(SLOTS):
                    if 1 <= t <= NB:
                        u = t - 1
                        act.wait_ge(pt_done, step + u + 1 + PRIME)
                        act.wait_ge(pv_done, step + u + PRIME)
                        act.copy(pt_hi[:], psum[:, BK_T, :].rearrange("p (a b) -> p a b", a=HG)
                                 ).then_inc(pthi_ready, 1)
                    if not more:
                        third_norm(t)
                    if t < NB:
                        act.wait_ge(neg_ready, step + t + 1)
                        for j in range(HG):
                            e = act.activation(probs[:, t % 2, j, :], probs[:, t % 2, j, :], ACT.Exp,
                                               bias=negmax[:, t % 2, j:j + 1], scale=SCALE,
                                               accum_out=rowsum[:, t % 2, j:j + 1])
                        e.then_inc(exp_done, 1)
                    if t in TURN_V and (more or TURN_V[t] == 1):
                        n = TURN_V[t]
                        act.wait_ge(vt_done, g * NH + (3 - n))
                        act.wait_ge(pv_done, step + (0 if n == 1 else BH) + PRIME)
                        v_first(n)
                    if not more:
                        context_first(t, 0)
                    for i in FILL[t]:
                        unit, n = BLOCKS[i]
                        if n == 0 and not more:
                            continue
                        act.wait_ge(proj_done, blocks + i + 1)
                        if unit == "v":
                            act.wait_ge(vt_done, g * NH + (2 - n))
                        else:
                            act.wait_ge(score_done, step + (0 if n == 1 else BH) + PRIME)
                        project_out(unit, n, BK_PROJ[i % 2])
                    if not more:
                        if t >= EARLY:
                            cross_exp(t)
                    if 1 <= t <= NB:
                        u = t - 1
                        act.wait_ge(pv_done, step + u + 1 + PRIME)
                        act.wait_ge(o_done, step + u - 1 + PRIME)
                        act.copy(at_hi[:, u % 2], psum[:, BK_PV, :].rearrange("p (a b) -> p a b", a=HG)
                                 ).then_inc(athi_ready, 1)
                    if not more:
                        if t < EARLY:
                            cross_exp(t)
                        third(t)
                        queries_out(t)
                        context_first(t, 1)
                        if t in EARLY_SECOND:
                            early_first(EARLY_SECOND[t])
                    for unit in SPLIT.get(t, ()):
                        if unit[0] == "o":
                            if unit == "o0":
                                act.wait_ge(ld_w["o"], g * 16 + 16)
                                act.wait_ge(o_done, step + PRIME)
                            split_first(unit)
                        elif more:
                            act.wait_ge(ld_w[unit[0]], g * 16 + 32)
                            act.wait_ge(proj_done, blocks + BLOCKS.index((unit, 1)) + 1)
                            split_first(unit)

            with act.Fori(0, LAST) as g:
                group(g, True)
            group(LAST, False)

            for t in range(SLOTS, ALL_SLOTS):
                cross_exp(t)
                third_norm(t)
                queries_out(t)
                third(t)
                if t in EARLY_SECOND:
                    early_first(EARLY_SECOND[t])

            def weight_first(unit, r, m, before, w):
                act.wait_ge(fw_ready, unit + 1)
                act.wait_ge(gu_done, before + PRIME)
                act.copy(f_hi[:, r, m, :, 0:w], f_w[:, m, :, 0:w]).then_inc(fhi_ready, 1)

            def tile_weights(n, r, w):
                for m in range(2):
                    weight_first(n * 2 + m, r, m, n * 2 + m - 3, w)

            def down_weights(c):
                w, r, m = width(c), (NT + c) % 2, (c // 2) % 2
                act.wait_ge(fw_ready, 2 * NT + c + 1)
                act.wait_ge(gu_done, (2 * (NT - 2 + c % 2) + m + 1 if c < 4 else 2 * NT + c - 3) + PRIME)
                act.copy(f_hi[0:w, r, m], f_w[0:w, c % 2]).then_inc(fhi_ready, 1)

            def inner(n, r, w):
                act.wait_ge(gu_done, n * 2 + 1 + PRIME)
                act.wait_ge(int_ready, n + PRIME)
                gate = psum[0:w, 4 * r:4 * r + 2, :].rearrange("p a b -> p (a b)")
                act.activation(f_sig[0:w, :], gate, ACT.Sigmoid).then_inc(sig_ready, 1)

            def inner_first(n, w):
                act.wait_ge(int_ready, n + 1 + PRIME)
                act.copy(int_hi[0:w, bass.ds(n, 1), :].rearrange("p a b -> p (a b)"),
                         f_int[0:w, :]).then_inc(inthi_ready, 1)

            inner(0, 0, P)
            tile_weights(2, 0, P)
            inner_first(0, P)
            inner(1, 1, P)
            inner_first(1, P)
            with act.Fori(0, (NT - 3 - EARLY_TILES) // 2) as pair:
                for r in range(2):
                    n = pair * 2 + EARLY_TILES + r
                    inner(n, r, P)
                    tile_weights(n + 1, 1 - r, P)
                    inner_first(n, P)
            for n in range(NT - 3, NT):
                inner(n, n % 2, width(n))
                if n + 1 < NT:
                    tile_weights(n + 1, (n + 1) % 2, width(n + 1))
                else:
                    down_weights(0)
                inner_first(n, width(n))
            for c in range(1, NT):
                down_weights(c)
            for b in range(NB):
                act.wait_ge(down_done, b + 1)
                if b >= 2:
                    act.wait_ge(y_ready, b - 1)
                act.copy(y16[:, b % 2, :], psum[:, b, :]).then_inc(y16_ready, 1)

        @block.gpsimd
        def _(pool):
            pool.memset(ident[:], 0.0).then_inc(consts_pool, 1)
            pool.memset(causal[:], 0.0).then_inc(consts_pool, 1)
            pool.wait_ge(consts_pool, 2)
            pool.affine_select(out=ident[:], in_=ident[:], compare_op=ALU.not_equal, fill=1.0,
                               base=0, pattern=[[-1, P]], channel_multiplier=1).then_inc(consts_pool, 1)
            pool.affine_select(out=causal[:], in_=causal[:], compare_op=ALU.is_ge, fill=MASKED,
                               base=0, pattern=[[-1, P]], channel_multiplier=1).then_inc(consts_pool, 1)
            pool.iota(part_i[:], pattern=[[0, 1]], base=0, channel_multiplier=1).then_inc(consts_pool, 1)
            pool.iota(z_shift[:], pattern=[[4, NIBBLES]], base=0, channel_multiplier=0).then_inc(consts_pool, 1)
            pool.sem_inc(intlo_ready, PRIME)

            pool.memset(halfneg[:], -0.5).then_inc(consts_pool, 1)
            pool.wait_ge(consts_pool, 7)
            steps = [0]

            def after(ins):
                steps[0] += 1
                ins.then_inc(rstd_step, 1)
                pool.wait_ge(rstd_step, steps[0])

            def inverse_deviation(b, k):
                v, r, n = vareps[:, b:b + 1], rstd[:, b:b + 1], newton[:, b:b + 1]
                pool.wait_ge(var_ready[k], b + 1)
                after(pool.tensor_scalar(v, meanvar[:, b, 1:2], EPS, 1.0, ALU.add, ALU.mult))
                after(pool.tensor_tensor(r, v, halfneg[:], ALU.pow))
                after(pool.tensor_tensor(n, r, r, ALU.mult))
                after(pool.tensor_tensor(n, n, v, ALU.mult))
                after(pool.tensor_scalar(n, n, -0.5, 1.5, ALU.mult, ALU.add))
                after(pool.tensor_tensor(r, r, n, ALU.mult))
                pool.tensor_scalar(shift[:, b:b + 1], meanvar[:, b, 0:1], r, -1.0, ALU.mult,
                                   ALU.mult).then_inc(rstd_ready[k], 1)

            def split_second(unit, count):
                hi, lo = weight(unit)
                pool.wait_ge(w_hi, count)
                pool.tensor_tensor(lo, weight(unit, raw=True), hi.bitcast(F32), ALU.subtract).then_inc(w_lo, 1)

            for b in range(NB):
                inverse_deviation(b, 0)
                if b >= BH:
                    split_second(HBLK[b - BH], b - BH + 1)
            for i in range(NB - BH, FIRST_UNITS):
                split_second(HBLK[i], i + 1)

            def group(g, more):
                step, n = g * NB, 0
                for t in range(SLOTS):
                    if t < NB:
                        pool.wait_ge(inv_ready, step + t + 1)
                        pool.tensor_tensor(probs[:, t % 2], probs[:, t % 2],
                                           rowinv[:, t % 2, :].unsqueeze(2).to_broadcast([P, HG, P]),
                                           ALU.mult).then_inc(prob_ready, 1)
                    for unit in SPLIT.get(t, ()):
                        if unit[0] == "o" or more:
                            n += 1
                            split_second(unit, g * UNITS + FIRST_UNITS + n)
                    if not more:
                        cross(t)
                        early(t)

            def cross(t):
                b = t - AT_NORM3 + (1 if t <= SLOTS else 2)
                if 0 <= b < NB:
                    inverse_deviation(b, 2)
                b = t - AT_NORM2 + 1
                if 0 <= b < NB:
                    inverse_deviation(b, 1)
                if t == SLOTS:
                    inverse_deviation(t - AT_NORM3 + 2, 2)

            def scaled(unit, m, r, w):
                pool.wait_ge(fm_ready, unit + 1)
                pool.tensor_tensor(f_w[:, m, :, 0:w], f_m[:, m, :, 0:w], f_s[:, r, m, :, 0:w],
                                   ALU.mult).then_inc(fw_ready, 1)

            def second(unit, m, r, w):
                pool.wait_ge(fhi_ready, unit + 1)
                pool.tensor_tensor(f_lo[:, r, m, :, 0:w], f_w[:, m, :, 0:w],
                                   f_hi[:, r, m, :, 0:w].bitcast(F32), ALU.subtract).then_inc(flo_ready, 1)

            def early(t):
                if t in EARLY_SECOND:
                    unit = EARLY_SECOND[t]
                    second(unit, unit % 2, unit // 2, P)
                if t in EARLY_SCALE:
                    unit = EARLY_SCALE[t]
                    if unit >= 2:
                        pool.wait_ge(flo_ready, unit - 1)
                    scaled(unit, unit % 2, unit // 2, P)

            with pool.Fori(0, LAST) as g:
                group(g, True)
            group(LAST, False)
            for t in range(SLOTS, ALL_SLOTS):
                cross(t)
                early(t)

            def tile_weights(n, r, w):
                for m in range(2):
                    pool.wait_ge(flo_ready, n * 2 + m - 1)
                    scaled(n * 2 + m, m, r, w)
                for m in range(2):
                    second(n * 2 + m, m, r, w)

            def down_weights(c):
                w, r, unit, m = width(c), (NT + c) % 2, 2 * NT + c, c % 2
                pool.wait_ge(fm_ready, unit + 1)
                pool.wait_ge(flo_ready, unit - 1)
                pool.tensor_tensor(f_w[0:w, m], f_m[0:w, m], f_s[0:w, r, 0], ALU.mult).then_inc(fw_ready, 1)
                pool.wait_ge(fhi_ready, unit + 1)
                k = (c // 2) % 2
                pool.tensor_tensor(f_lo[0:w, r, k], f_w[0:w, m], f_hi[0:w, r, k].bitcast(F32),
                                   ALU.subtract).then_inc(flo_ready, 1)

            def inner_second(n, w):
                pool.wait_ge(inthi_ready, n + 1)
                at = bass.ds(n, 1)
                pool.tensor_tensor(int_lo[0:w, at, :].rearrange("p a b -> p (a b)"), f_int[0:w, :],
                                   int_hi[0:w, at, :].rearrange("p a b -> p (a b)").bitcast(F32),
                                   ALU.subtract).then_inc(intlo_ready, 1)

            tile_weights(2, 0, P)
            inner_second(0, P)
            inner_second(1, P)
            with pool.Fori(0, (NT - 3 - EARLY_TILES) // 2) as pair:
                for r in range(2):
                    n = pair * 2 + EARLY_TILES + r
                    tile_weights(n + 1, 1 - r, P)
                    inner_second(n, P)
            for n in range(NT - 3, NT):
                if n + 1 < NT:
                    tile_weights(n + 1, (n + 1) % 2, width(n + 1))
                else:
                    down_weights(0)
                inner_second(n, width(n))
            for c in range(1, NT):
                down_weights(c)

        @block.vector
        def _(dve):
            for s in (masked, ptlo_ready, atlo_ready, o_added, int_ready):
                dve.sem_inc(s, PRIME)
            steps = [0]

            def after(ins):
                steps[0] += 1
                ins.then_inc(stat_step, 1)
                dve.wait_ge(stat_step, steps[0])

            def count(b, k):
                after(dve.bn_stats(stats[:, b, :], xacc[:, b, :]))
                dve.bn_aggr(meanvar[:, b, :], stats[:, b, :]).then_inc(var_ready[k], 1)

            def tile_second(b, k, hi, lo, bank):
                dve.wait_ge(ln_hi[k], b + 1)
                cols = slice(b * P, (b + 1) * P)
                dve.tensor_tensor(lo[:, :, cols], psum[:, bank, :].rearrange("p (c t) -> p c t", c=HC),
                                  hi[:, :, cols].bitcast(F32), ALU.subtract).then_inc(ln_lo[k], 1)

            for i in range(NB + 2):
                if i < NB:
                    dve.wait_ge(ld_x[i], 16)
                    count(i, 0)
                if i >= 2:
                    tile_second(i - 2, 0, xt_hi, xt_lo, (BK_T, BK_VT)[i % 2])
            dve.wait_ge(consts_pool, 7)
            dve.tensor_scalar(q_shift[:], part_i[:], NIBBLES - 1, 2, ALU.bitwise_and,
                              ALU.logical_shift_left).then_inc(consts_dve, 1)

            def v_second(n):
                dve.tensor_tensor(v_lo[:, n * BH:(n + 1) * BH, :],
                                  psum[:, BK_VT, :].rearrange("p (a b) -> p a b", a=BH),
                                  v_hi[:, n * BH:(n + 1) * BH, :].bitcast(F32),
                                  ALU.subtract).then_inc(vt_lo, 1)

            dve.wait_ge(vt_hi, 1)
            v_second(0)

            def cross_max(t):
                b = t - AT_SIM
                if 0 <= b < NB:
                    r = slice(b % 2, b % 2 + 1)
                    dve.wait_ge(xs_done, b + 1)
                    dve.tensor_reduce(xmax[:, r], psum[:, BK_XS, 0:P], AX_X, ALU.max).then_inc(xs_max, 1)
                    dve.wait_ge(xs_max, b + 1)
                    dve.tensor_scalar(xneg[:, r], xmax[:, r], -SCALE, None, ALU.mult).then_inc(xs_neg, 1)

            def cross_inverse(t):
                b = t - AT_SIM
                if 0 <= b < NB:
                    r = slice(b % 2, b % 2 + 1)
                    dve.wait_ge(xs_exp, b + 1)
                    dve.reciprocal(xinv[:, r], xsum[:, r]).then_inc(xs_inv, 1)
                    dve.wait_ge(xs_inv, b + 1)
                    dve.tensor_scalar(xprobs[:, b % 2, :], xprobs[:, b % 2, :], xinv[:, r], None,
                                      ALU.mult).then_inc(xs_prob, 1)

            def third_second(t):
                b = t - AT_NORM3
                if 0 <= b < NB:
                    tile_second(b, 2, ft_hi, ft_lo, BK_FT)

            def add_heads(g, u):
                dve.wait_ge(o_done, g * NB + u + 1 + PRIME)
                dve.tensor_tensor(xacc[:, u, :], psum[:, BK_O, :], xacc[:, u, :],
                                  ALU.add).then_inc(o_added, 1)

            def early_unpack(t):
                if t in EARLY_UNPACK:
                    n, m = divmod(EARLY_UNPACK[t], 2)
                    unpack(m, n % 2, P, (n // 2 + 1) * TILE_LOADS, 2 * n + m, 3 * (2 * n + m), n + m > 0)

            def add_and_count(g, u):
                add_heads(g, u)
                dve.wait_ge(o_added, g * NB + u + 1 + PRIME)
                count(u, 1)

            def cross_last(t):
                b = t - AT_NORM3 + 1
                if 0 <= b < NB:
                    dve.wait_ge(xc_done, b + 1)
                    dve.tensor_tensor(xacc[:, b, :], psum[:, BK_XC, :], xacc[:, b, :],
                                      ALU.add).then_inc(x_added, 1)
                    dve.wait_ge(x_added, b + 1)
                    count(b, 2)

            def group(g, more):
                step = g * NB
                for t in range(SLOTS + 1 if more else SLOTS):
                    if t < NB:
                        r = t % 2
                        dve.wait_ge(score_done, step + t + 1 + PRIME)
                        dve.wait_ge(pt_done, step + t - 1 + PRIME)
                        dve.tensor_tensor(probs[:, r], psum[:, BK_S, :].rearrange("p (a b) -> p a b", a=HG),
                                          causal[:].unsqueeze(1).to_broadcast([P, HG, P]),
                                          ALU.add).then_inc(masked, 1)
                        dve.wait_ge(masked, step + t + 1 + PRIME)
                        dve.tensor_reduce(rowmax[:, r, :], probs[:, r], AX_X, ALU.max).then_inc(maxed, 1)
                        dve.wait_ge(maxed, step + t + 1)
                        dve.tensor_scalar(negmax[:, r, :], rowmax[:, r, :], -SCALE, None,
                                          ALU.mult).then_inc(neg_ready, 1)
                    if 1 <= t <= NB:
                        u = t - 1
                        dve.wait_ge(pthi_ready, step + u + 1)
                        dve.tensor_tensor(pt_lo[:], psum[:, BK_T, :].rearrange("p (a b) -> p a b", a=HG),
                                          pt_hi[:].bitcast(F32), ALU.subtract).then_inc(ptlo_ready, 1)
                    if not more:
                        cross_max(t)
                    if t >= 3 and (more or t < EARLY):
                        add_heads(g, t - 3)
                    if t < NB:
                        dve.wait_ge(exp_done, step + t + 1)
                        dve.reciprocal(rowinv[:, t % 2, :], rowsum[:, t % 2, :]).then_inc(inv_ready, 1)
                    if not more:
                        cross_inverse(t)
                        if t > AT_SIM:
                            cross_last(t)
                        if t == EARLY - 1:
                            dve.wait_ge(o_added, step + t - 2 + PRIME)
                            count(t - 3, 1)
                        if t >= EARLY:
                            add_and_count(g, t - 2)
                    if t in TURN_V and (more or TURN_V[t] == 1):
                        dve.wait_ge(vt_hi, g * NH + (3 - TURN_V[t]))
                        v_second(TURN_V[t])
                    if not more and t < EARLY:
                        early_unpack(t)
                    if 1 <= t <= NB:
                        u = t - 1
                        dve.wait_ge(athi_ready, step + u + 1)
                        dve.tensor_tensor(at_lo[:, u % 2], psum[:, BK_PV, :].rearrange("p (a b) -> p a b", a=HG),
                                          at_hi[:, u % 2].bitcast(F32), ALU.subtract).then_inc(atlo_ready, 1)
                    if not more:
                        if t == EARLY - 1:
                            add_and_count(g, t - 2)
                        third_second(t)
                        if t >= EARLY:
                            early_unpack(t)

            dve.wait_ge(consts_dve, 1)
            TILE_LOADS = 16 * 2 * (HC + 2)
            DOWN_LOADS = 16 * 3

            def unpack(m, r, w, loads, unit, group_step, free, down=False):
                dve.wait_ge(ld_f[r], loads)
                if down:
                    q, z = f_q[0:w, r, 0], f_z[0:w, r, 0].rearrange("p a b -> p (a b)")
                    zn, dst = f_zn[0:w].rearrange("p a b -> p (a b)"), f_m[0:w, m]
                    zb = z.unsqueeze(2).to_broadcast([w, H // NIBBLES, NIBBLES])
                    zo = zn.rearrange("p (a b) -> p a b", b=NIBBLES)
                    sh = z_shift[0:w].unsqueeze(1).to_broadcast([w, H // NIBBLES, NIBBLES])
                    zn = f_zn[0:w]
                    rows = w
                else:
                    zw = w // NIBBLES
                    q, z = f_q[:, r, m, :, 0:w], f_z[:, r, m, :, 0:zw]
                    zn, dst = f_zn[:, :, 0:w], f_m[:, m, :, 0:w]
                    zb = z.unsqueeze(3).to_broadcast([P, HC, zw, NIBBLES])
                    zo = zn.rearrange("p c (a b) -> p c a b", b=NIBBLES)
                    sh = z_shift[:].unsqueeze(1).unsqueeze(1).to_broadcast([P, HC, zw, NIBBLES])
                    rows = P
                if free:
                    dve.wait_ge(fm_ready, unit)
                dve.tensor_scalar(q, q, q_shift[0:rows, 0:1], 15, ALU.logical_shift_right,
                                  ALU.bitwise_and).then_inc(fq_step, 1)
                dve.tensor_tensor(zo, zb, sh, ALU.logical_shift_right).then_inc(fq_step, 1)
                dve.wait_ge(fq_step, group_step + 2)
                dve.tensor_scalar(zn, zn, 15, None, ALU.bitwise_and).then_inc(fq_step, 1)
                dve.wait_ge(fq_step, group_step + 3)
                if not isinstance(unit, int) or unit >= 2:
                    dve.wait_ge(fw_ready, unit - 1)
                dve.scalar_tensor_tensor(dst, q, -1.0, zn, ALU.add, ALU.subtract).then_inc(fm_ready, 1)

            with dve.Fori(0, LAST) as g:
                group(g, True)
            group(LAST, False)

            for t in range(SLOTS, ALL_SLOTS):
                cross_max(t)
                cross_inverse(t)
                if t == SLOTS:
                    cross_last(t)
                cross_last(t + 1)
                third_second(t)
            for m in range(2):
                unpack(m, 0, P, 2 * TILE_LOADS, 4 + m, 3 * (4 + m), True)

            def tile_weights(n, r, w, uses):
                for m in range(2):
                    unpack(m, r, w, uses * TILE_LOADS + TILE_LOADS, n * 2 + m, n * 6 + 3 * m, True)

            def down_weights(c):
                r = (NT + c) % 2
                tiles = (NT + 1 - r) // 2
                loads = tiles * TILE_LOADS + (c // 2 + 1) * DOWN_LOADS
                unpack(c % 2, r, width(c), loads, 2 * NT + c, 6 * NT + 3 * c, True, down=True)

            def inner(n, r, w):
                gate = psum[0:w, 4 * r:4 * r + 2, :].rearrange("p a b -> p (a b)")
                up = psum[0:w, 4 * r + 2:4 * r + 4, :].rearrange("p a b -> p (a b)")
                dve.wait_ge(sig_ready, n + 1)
                dve.tensor_tensor(f_sig[0:w, :], gate, f_sig[0:w, :], ALU.mult).then_inc(gs_ready, 1)
                dve.wait_ge(gs_ready, n + 1)
                dve.wait_ge(gu_done, n * 2 + 2 + PRIME)
                dve.wait_ge(intlo_ready, n + PRIME)
                dve.tensor_tensor(f_int[0:w, :], up, f_sig[0:w, :], ALU.mult).then_inc(int_ready, 1)

            for n in range(EARLY_TILES):
                inner(n, n, P)
                unpack(n, 1, P, 2 * TILE_LOADS, 6 + n, 3 * (6 + n), True)
            with dve.Fori(0, (NT - 3 - EARLY_TILES) // 2) as pair:
                for r in range(2):
                    n = pair * 2 + EARLY_TILES + r
                    tile_weights(n + 2, r, P, pair + 2)
                    inner(n, r, P)
            for n in range(NT - 3, NT):
                if n + 2 < NT:
                    tile_weights(n + 2, n % 2, width(n + 2), (n + 2) // 2)
                else:
                    down_weights(n + 2 - NT)
                inner(n, n % 2, width(n))
            for c in range(2, NT):
                down_weights(c)
            for b in range(NB):
                dve.wait_ge(y16_ready, b + 1)
                dve.tensor_tensor(xacc[:, b, :], xacc[:, b, :], y16[:, b % 2, :], ALU.add).then_inc(y_ready, 1)


_INS = ["x", "ctx_4096", "L0_attn_w_q", "L0_attn_w_k", "L0_attn_w_v", "L0_attn_w_o",
        "L0_ffn_gate_qweight", "L0_ffn_gate_scales", "L0_ffn_gate_zeros",
        "L0_ffn_up_qweight", "L0_ffn_up_scales", "L0_ffn_up_zeros",
        "L0_ffn_down_qweight", "L0_ffn_down_scales", "L0_ffn_down_zeros"]


def kernel(**inputs):
    import numpy as np
    import concourse.bacc as bacc
    from concourse.bass_utils import run_bass_kernel_spmd

    nc = bacc.Bacc("TRN2", target_bir_lowering=False, num_devices=1)
    arrays, args = {}, []
    for name in _INS:
        a = np.ascontiguousarray(inputs[name])
        arrays[f"in_{name}"] = a
        args.append(nc.dram_tensor(f"in_{name}", a.shape, mybir.dt.from_np(a.dtype), kind="ExternalInput").ap())
    shape = inputs["x"].shape
    args.append(nc.dram_tensor("out_0", shape, F32, kind="ExternalOutput").ap())
    decoder_kernel(nc, *args)
    got = run_bass_kernel_spmd(nc, [arrays], core_ids=[0])
    return got.results[0]["out_0"]
```
